# Optimizing a Trainium2 kernel written in Bass

```python
import numpy as np
import jax
import jax.numpy as jnp

def _softmax(x, axis=-1):
    return jax.nn.softmax(x, axis=axis)

def _gelu(x):
    return jax.nn.gelu(x, approximate=True)

def _silu(x):
    return jax.nn.silu(x)

def _sigmoid(x):
    return jax.nn.sigmoid(x)

def _layernorm(x, axis=-1, eps=1e-05):
    m = jnp.mean(x, axis=axis, keepdims=True)
    v = jnp.var(x, axis=axis, keepdims=True)
    return (x - m) / jnp.sqrt(v + eps)

def _scatter_add(tgt, idx, src, axis=0):
    return tgt.at[idx].add(src)

def _segment_sum(src, seg, n):
    return jax.ops.segment_sum(src, seg, n)
kernel_name = 'mk_prb_d1_jaxref_r4_77c99b'

def setup_inputs(seed: int=0):
    np.random.seed(seed)
    _w = jnp.asarray

    def _L0_attn_setup():
        import jax, jax.numpy as jnp
        import numpy as np
        B, N, D = (2, 512, 256)
        H, WS = (16, 128)
        DH = D // H
        HALF = WS // 2
        key = jax.random.key(seed)
        ks = jax.random.split(key, 5)
        return {'x': jax.random.normal(ks[0], (B, N, D), dtype=jnp.float32), 'Wqkv': jax.random.normal(ks[1], (D, 3 * D), dtype=jnp.float32) * 0.02, 'bqkv': jax.random.normal(ks[2], (3 * D,), dtype=jnp.float32) * 0.02, 'Wout': jax.random.normal(ks[3], (D, D), dtype=jnp.float32) * 0.02, 'bout': jax.random.normal(ks[4], (D,), dtype=jnp.float32) * 0.02}
    _L0_attn_in = _L0_attn_setup()

    def _L0_ffn_setup():
        import jax, jax.numpy as jnp
        import numpy as np
        NEG_INF = -1e+30

        def _moe_forward(x, router_w, router_b, w1, b1, w2, b2, top_k=2):
            B, S, D = x.shape
            E = router_w.shape[1]
            logits = jnp.einsum('bsd,de->bse', x, router_w) + router_b
            top_vals, top_idx = jax.lax.top_k(logits, top_k)
            keep = jax.nn.one_hot(top_idx, E, dtype=logits.dtype).sum(-2) > 0
            sparse_logits = jnp.where(keep, logits, NEG_INF)
            gating = jax.nn.softmax(sparse_logits, axis=-1)
            xf = x.reshape(-1, D)
            gf = gating.reshape(-1, E)
            h = jax.nn.relu(jnp.einsum('td,edh->eth', xf, w1) + b1[:, None, :])
            y = jnp.einsum('eth,ehd->etd', h, w2) + b2[:, None, :]
            out = jnp.einsum('etd,te->td', y, gf)
            return out.reshape(B, S, D)
        key = jax.random.key(seed)
        ks = jax.random.split(key, 5)
        B, S, D, E, H = (2, 512, 256, 8, 1024)
        scale = 0.02
        return {'x': jax.random.normal(ks[0], (B, S, D), dtype=jnp.float32), 'router_w': jax.random.normal(ks[1], (D, E), dtype=jnp.float32) * scale, 'router_b': jnp.zeros((E,), dtype=jnp.float32), 'w1': jax.random.normal(ks[2], (E, D, H), dtype=jnp.float32) * scale, 'b1': jnp.zeros((E, H), dtype=jnp.float32), 'w2': jax.random.normal(ks[3], (E, H, D), dtype=jnp.float32) * scale, 'b2': jnp.zeros((E, D), dtype=jnp.float32)}
    _L0_ffn_in = _L0_ffn_setup()
    _d = {'L0_attn_x': _L0_attn_in['x'], 'L0_attn_Wqkv': _L0_attn_in['Wqkv'], 'L0_attn_bqkv': _L0_attn_in['bqkv'], 'L0_attn_Wout': _L0_attn_in['Wout'], 'L0_attn_bout': _L0_attn_in['bout'], 'L0_ffn_router_w': _L0_ffn_in['router_w'], 'L0_ffn_router_b': _L0_ffn_in['router_b'], 'L0_ffn_w1': _L0_ffn_in['w1'], 'L0_ffn_b1': _L0_ffn_in['b1'], 'L0_ffn_w2': _L0_ffn_in['w2'], 'L0_ffn_b2': _L0_ffn_in['b2']}
    _x0 = _d['L0_attn_x']
    _d['L0_attn_x'] = jax.random.normal(jax.random.fold_in(jax.random.key(seed), 1), (8, 512, 256), dtype=_x0.dtype)
    del _x0
    return _d

def reference(L0_attn_x, L0_attn_Wqkv, L0_attn_bqkv, L0_attn_Wout, L0_attn_bout, L0_ffn_router_w, L0_ffn_router_b, L0_ffn_w1, L0_ffn_b1, L0_ffn_w2, L0_ffn_b2):

    def _L0_attn_ref(x, Wqkv, bqkv, Wout, bout):
        import jax, jax.numpy as jnp
        import numpy as np
        B, N, D = (2, 512, 256)
        H, WS = (16, 128)
        DH = D // H
        HALF = WS // 2
        b, n, d = x.shape
        scale = DH ** (-0.5)
        qkv = x @ Wqkv + bqkv
        q, k, v = jnp.split(qkv, 3, axis=-1)

        def heads(t):
            return t.reshape(b, n, H, DH).transpose(0, 2, 1, 3)
        q, k, v = (heads(q), heads(k), heads(v))
        scores = jnp.einsum('bhid,bhjd->bhij', q, k) * scale
        idx = jnp.arange(n)
        band = jnp.abs(idx[:, None] - idx[None, :]) <= HALF
        neg = jnp.asarray(jnp.finfo(scores.dtype).min, scores.dtype)
        scores = jnp.where(band[None, None], scores, neg)
        attn = jax.nn.softmax(scores, axis=-1)
        out = jnp.einsum('bhij,bhjd->bhid', attn, v)
        out = out.transpose(0, 2, 1, 3).reshape(b, n, d)
        return out @ Wout + bout

    def _L0_ffn_ref(x, router_w, router_b, w1, b1, w2, b2):
        import jax, jax.numpy as jnp
        import numpy as np
        NEG_INF = -1e+30

        def _moe_forward(x, router_w, router_b, w1, b1, w2, b2, top_k=2):
            B, S, D = x.shape
            E = router_w.shape[1]
            logits = jnp.einsum('bsd,de->bse', x, router_w) + router_b
            top_vals, top_idx = jax.lax.top_k(logits, top_k)
            keep = jax.nn.one_hot(top_idx, E, dtype=logits.dtype).sum(-2) > 0
            sparse_logits = jnp.where(keep, logits, NEG_INF)
            gating = jax.nn.softmax(sparse_logits, axis=-1)
            xf = x.reshape(-1, D)
            gf = gating.reshape(-1, E)
            h = jax.nn.relu(jnp.einsum('td,edh->eth', xf, w1) + b1[:, None, :])
            y = jnp.einsum('eth,ehd->etd', h, w2) + b2[:, None, :]
            out = jnp.einsum('etd,te->td', y, gf)
            return out.reshape(B, S, D)
        return _moe_forward(x, router_w, router_b, w1, b1, w2, b2, top_k=2)
    x = L0_attn_x
    xn = _layernorm(x, axis=-1)
    x = x + _L0_attn_ref(xn, L0_attn_Wqkv, L0_attn_bqkv, L0_attn_Wout, L0_attn_bout) + _L0_ffn_ref(xn, L0_ffn_router_w, L0_ffn_router_b, L0_ffn_w1, L0_ffn_b1, L0_ffn_w2, L0_ffn_b2)
    return x

_drawn_inputs = setup_inputs


def setup_inputs(seed=0):
    import zlib

    import numpy as np

    out = dict(_drawn_inputs(seed))
    spreads = {'L0_ffn_router_b': (0.0, 0.303), 'L0_ffn_b1': (0.0, 0.537), 'L0_ffn_b2': (0.0, 0.1)}
    factors = {'L0_attn_Wqkv': 6.085, 'L0_attn_bqkv': 7.665, 'L0_attn_Wout': 5.009, 'L0_attn_bout': 2.933}
    for name, (base, spread) in spreads.items():
        noise = np.random.default_rng([zlib.crc32(name.encode()), seed]).standard_normal(out[name].shape)
        drawn = base * np.exp(spread * noise) if base else spread * noise
        out[name] = jnp.asarray(drawn.astype(out[name].dtype))
    for name, factor in factors.items():
        out[name] = (out[name] * factor).astype(out[name].dtype)
    return out
```

```python
from contextlib import ExitStack

import concourse.bass as bass
from concourse import mybir
from concourse.alu_op_type import AluOpType as ALU

F32 = mybir.dt.float32
F32R = mybir.dt.float32r
BF16 = mybir.dt.bfloat16
I32 = mybir.dt.int32
U32 = mybir.dt.uint32
ACT = mybir.ActivationFunctionType
AX = mybir.AxisListType.X

P = 128
B, N, D = 8, 512, 256
T = B * N
H, DH = 16, 16
HALF = 64
E, F = 8, 1024
DC = D // P
FC = F // P
TB = N // P
NT = T // P
VT = TB + 1
HC = P // DH
ROWS = 2 * P
STEPS = 2 * T // ROWS + E
SLOTS = STEPS * ROWS
HT = SLOTS // P
EPS = 1e-5
FAR = 3.0e38
ds = bass.ds


class Shared:

    def __init__(self, inputs):
        self.x, self.Wqkv, self.bqkv, self.bqk_cols = (inputs[n] for n in ("x", "Wqkv", "bqkv", "bqk_cols"))
        self.Wout, self.bout = inputs["Wout"], inputs["bout"]
        self.router_w, self.router_b = inputs["router_w"], inputs["router_b"]
        self.w1, self.b1_cols, self.w2, self.b2 = (inputs[n] for n in ("w1", "b1_cols", "w2", "b2"))


START = 1


def start(eng, sems):
    for sem in sems:
        eng.sem_inc(sem, START)


def wait(eng, sem, count):
    eng.wait_ge(sem, count + START)


class Chain:

    def __init__(self, eng, sem, base=0):
        self.eng, self.sem, self.count, self.base = eng, sem, 0, base

    def add(self, ins, inc=1):
        ins.then_inc(self.sem, inc)
        self.count += inc
        return self

    def value(self):
        return self.base + self.count

    def wait(self):
        wait(self.eng, self.sem, self.value())


def wait_first(eng, sem, value, tick):
    wait(eng, sem, value)
    eng.sem_inc(tick, 1)


def norm_project(nc, g):
    with ExitStack() as ctx:
        def sb(name, shape, dt=F32):
            return ctx.enter_context(nc.sbuf_tensor(name, shape, dt))

        by = {"sp": [], "pool": [], "v": [], "act": [], "pe": []}

        def sem(name, engine):
            by[engine].append(ctx.enter_context(nc.semaphore(name)))
            return by[engine][-1]

        ps = ctx.enter_context(nc.psum_tensor("ps_project", [P, 8, 512], F32))
        w_raw = sb("w_raw", [P, DC, 3 * D])
        w_hi = sb("w_hi", [P, DC, 3 * D], F32R)
        w_lo = sb("w_lo", [P, DC, 3 * D], F32R)
        rw_raw = sb("rw_raw", [P, DC, E])
        rw = sb("rw", [P, DC, 2 * E], F32R)
        rb = sb("rb", [P, E])
        b_qk = sb("b_qk", [P, 2 * DC])
        b_v = sb("b_v", [P, D])
        x = sb("x_in", [P, 2, TB, D])
        xn = sb("xn", [P, 2, TB, D])
        stats = sb("stats", [P, TB, 6])
        mv = sb("mv", [P, TB, 2])
        var = sb("var", [P, TB])
        root = sb("root", [P, TB])
        rough = sb("rough", [P, TB])
        newton = sb("newton", [P, TB])
        rstd = sb("rstd", [P, TB])
        xt_hi = sb("xt_hi", [P, 2, DC, N + 2 * HALF], F32R)
        xt_lo = sb("xt_lo", [P, 2, DC, N + 2 * HALF], F32R)
        lg = sb("lg", [P, TB, E])

        s_w = sem("s_w", "sp")
        s_whi = sem("s_whi", "act")
        s_wlo = sem("s_wlo", "v")
        s_ident = sem("s_ident", "pool")
        s_x = sem("s_x", "sp")
        s_dve = sem("s_dve", "v")
        s_var = sem("s_var", "v")
        s_root = sem("s_root", "act")
        s_tick = sem("s_tick", "v")
        s_xn = sem("s_xn", "v")
        s_xnout = sem("s_xnout", "sp")
        s_tr = sem("s_tr", "pe")
        s_hi = sem("s_hi", "act")
        s_lo = sem("s_lo", "v")
        s_lg = sem("s_lg", "pe")
        s_lgout = sem("s_lgout", "v")
        s_qk = sem("s_qk", "pe")
        s_qout = sem("s_qout", "act")
        s_kout = sem("s_kout", "v")
        s_v = sem("s_v", "pe")
        s_vout = sem("s_vout", "v")
        s_pad = sem("s_pad", "v")

        bank_t, bank_l, bank_qk, bank_v = (0, 1), 2, (3, 4), (5, 6, 7)
        v_banks = [(0, 1), (2, 3), (4,)]
        x_rows = g.x.rearrange("b (t p) d -> b p t d", p=P)
        xn_rows = g.xn_dram.rearrange("(b t p) d -> b p t d", t=TB, p=P)

        with nc.Block() as block:
            @block.sync
            def _(sp):
                start(sp, by["sp"])
                sp.dma_start(w_raw[:], g.Wqkv.rearrange("(c p) n -> p c n", p=P)).then_inc(s_w, 16)
                sp.dma_start(rw_raw[:], g.router_w.rearrange("(c p) e -> p c e", p=P)).then_inc(s_w, 16)
                sp.dma_start(rb[:], g.router_b.partition_broadcast(P)).then_inc(s_w, 16)
                sp.dma_start(b_qk[:], g.bqk_cols).then_inc(s_w, 16)
                sp.dma_start(b_v[:], g.bqkv[2 * D:3 * D].partition_broadcast(P)).then_inc(s_w, 16)

                def load(b, par):
                    sp.dma_start(x[:, par], x_rows[ds(b, 1)].rearrange("b p t d -> (b p) t d")
                                 ).then_inc(s_x, 16)

                load(0, 0)
                with sp.Fori(0, B // 2) as pair:
                    for par in range(2):
                        b = 2 * pair + par
                        following = (b + 1) % B
                        wait_first(sp, s_x, 16 * b + 16, g.tick)
                        wait_first(sp, s_xn, b, g.tick)
                        load(following, 1 - par)
                        wait_first(sp, s_xn, b + 1, g.tick)
                        wait_first(sp, s_xnout, 16 * b, g.tick)
                        sp.dma_start(xn_rows[ds(b, 1)].rearrange("b p t d -> (b p) t d"),
                                     xn[:, par]).then_inc(s_xnout, 16)
                wait(sp, s_xnout, 16 * B)
                wait(sp, s_x, 16 * (B + 1))

            @block.gpsimd
            def _(pool):
                start(pool, by["pool"])
                pool.memset(g.ident[:], 0.0).then_inc(s_ident, 1)
                wait(pool, s_ident, 1)
                pool.affine_select(out=g.ident[:], in_=g.ident[:], compare_op=ALU.not_equal, fill=1.0,
                                   base=0, pattern=[[-1, P]], channel_multiplier=1).then_inc(s_ident, 1)
            @block.vector
            def _(v):
                start(v, by["v"])
                for buf in (xt_hi, xt_lo):
                    for par in range(2):
                        for c in range(DC):
                            v.memset(buf[:, par, c, 0:HALF].bitcast(F32), 0.0).then_inc(s_pad, 1)
                            v.memset(buf[:, par, c, N + HALF:N + 2 * HALF].bitcast(F32), 0.0).then_inc(s_pad, 1)
                wait(v, s_whi, 2)
                v.tensor_tensor(w_lo[:], w_raw[:], w_hi[:].bitcast(F32), ALU.subtract).then_inc(s_wlo, 1)
                v.tensor_tensor(rw[:, :, E:2 * E], rw_raw[:], rw[:, :, 0:E].bitcast(F32),
                                ALU.subtract).then_inc(s_wlo, 1)
                with v.Fori(0, B // 2) as pair:
                    for par in range(2):
                        b = 2 * pair + par
                        chain = Chain(v, s_dve, 8 * b)
                        wait(v, s_x, 16 * (b + 1))
                        for t in range(TB):
                            ins = v.bn_stats(stats[:, t, :], x[:, par, t, :])
                        chain.add(ins)
                        wait_first(v, s_dve, chain.value(), s_tick)
                        for t in range(TB):
                            ins = v.bn_aggr(mv[:, t, :], stats[:, t, :])
                        chain.add(ins).wait()
                        v.tensor_scalar(var[:], mv[:, :, 1], EPS, None, ALU.add).then_inc(s_var, 1)
                        wait(v, s_root, b + 1)
                        chain.add(v.reciprocal(rough[:], root[:])).wait()
                        chain.add(v.tensor_tensor(newton[:], rough[:], rough[:], ALU.mult)).wait()
                        chain.add(v.tensor_tensor(newton[:], newton[:], var[:], ALU.mult)).wait()
                        chain.add(v.tensor_scalar(newton[:], newton[:], -0.5, 1.5, ALU.mult, ALU.add)).wait()
                        chain.add(v.tensor_tensor(rstd[:], rough[:], newton[:], ALU.mult)).wait()
                        wait(v, s_tr, 2 * b)
                        wait(v, s_xnout, 16 * b)
                        for t in range(TB):
                            ins = v.tensor_scalar(xn[:, par, t, :], x[:, par, t, :], mv[:, t, 0:1],
                                                  rstd[:, t:t + 1], ALU.subtract, ALU.mult)
                        ins.then_inc(s_xn, 1)
                        for c in range(DC):
                            wait(v, s_hi, 2 * b + c + 1)
                            v.tensor_tensor(xt_lo[:, par, c, HALF:HALF + N], ps[:, bank_t[c], :],
                                            xt_hi[:, par, c, HALF:HALF + N].bitcast(F32),
                                            ALU.subtract).then_inc(s_lo, 1)
                        wait(v, s_lg, b + 1)
                        lg_ps = ps[:, bank_l, 0:TB * 2 * E].rearrange("p (t e) -> p t e", t=TB)
                        chain.add(v.tensor_tensor(lg[:], lg_ps[:, :, E:2 * E],
                                                  rb[:].unsqueeze(1).to_broadcast([P, TB, E]), ALU.add)
                                  ).wait()
                        v.tensor_tensor(g.logits[:, ds(b * TB, TB), :], lg_ps[:, :, 0:E], lg[:], ALU.add
                                        ).then_inc(s_lgout, 1)
                        for m in (2, 3):
                            wait(v, s_qk, 4 * b + m + 1)
                            v.tensor_scalar(g.k_of(b, m - 2), ps[:, bank_qk[m % 2], :], b_qk[:, m:m + 1],
                                            None, ALU.add).then_inc(s_kout, 1)
                        for n, tiles in enumerate(v_banks):
                            wait(v, s_v, 3 * b + n + 1)
                            tiles_ps = ps[:, bank_v[n], 0:D * len(tiles)].rearrange("p (t d) -> p t d", d=D)
                            for c in range(DC):
                                ins = v.tensor_tensor(
                                    g.v_of(b, c, tiles[0], len(tiles)), tiles_ps[:, :, c * P:(c + 1) * P],
                                    b_v[:, c * P:(c + 1) * P].unsqueeze(1).to_broadcast([P, len(tiles), P]),
                                    ALU.add)
                            ins.then_inc(s_vout, 1)
                wait(v, s_vout, 3 * B)

            @block.scalar
            def _(act):
                start(act, by["act"])
                wait(act, s_w, 80)
                act.activation(w_hi[:], w_raw[:], ACT.Copy).then_inc(s_whi, 1)
                act.activation(rw[:, :, 0:E], rw_raw[:], ACT.Copy).then_inc(s_whi, 1)
                with act.Fori(0, B // 2) as pair:
                    for par in range(2):
                        b = 2 * pair + par
                        wait(act, s_var, b + 1)
                        act.activation(root[:], var[:], ACT.Sqrt).then_inc(s_root, 1)
                        for c in range(DC):
                            wait(act, s_tr, 2 * b + c + 1)
                            act.activation(xt_hi[:, par, c, HALF:HALF + N], ps[:, bank_t[c], :],
                                           ACT.Copy).then_inc(s_hi, 1)
                        for m in (0, 1):
                            wait(act, s_qk, 4 * b + m + 1)
                            act.activation(g.q_of(b, m), ps[:, bank_qk[m % 2], :], ACT.Identity,
                                           bias=b_qk[:, m:m + 1]).then_inc(s_qout, 1)

            @block.tensor
            def _(pe):
                start(pe, by["pe"])
                wait(pe, s_ident, 2)
                wait(pe, s_wlo, 2)
                wait(pe, s_pad, 16)
                with pe.Fori(0, B // 2) as pair:
                    for par in range(2):
                        b = 2 * pair + par
                        wait(pe, s_xn, b + 1)
                        wait(pe, s_lo, 2 * b)
                        for c in range(DC):
                            for t in range(TB):
                                ins = pe.transpose(ps[:, bank_t[c], t * P:(t + 1) * P],
                                                   xn[:, par, t, c * P:(c + 1) * P], g.ident[:])
                            ins.then_inc(s_tr, 1)
                        hi, lo = xt_hi[:, par], xt_lo[:, par]
                        wait(pe, s_lo, 2 * b + 2)
                        for m in range(4):
                            if m < 2:
                                wait(pe, s_kout, 2 * b)
                            else:
                                wait(pe, s_qout, 2 * b + m - 1)
                            n = 0
                            for c in range(DC):
                                for w, xx in ((w_hi, hi), (w_hi, lo), (w_lo, hi)):
                                    ins = pe.matmul(ps[:, bank_qk[m % 2], :], w[:, c, m * P:(m + 1) * P],
                                                    xx[:, c, HALF:HALF + N], start=(n == 0), stop=(n == 5))
                                    n += 1
                            ins.then_inc(s_qk, 1)
                        wait(pe, s_lgout, b)
                        for t in range(TB):
                            n = 0
                            for c in range(DC):
                                for xx in (hi, lo):
                                    ins = pe.matmul(ps[:, bank_l, t * 2 * E:(t + 1) * 2 * E],
                                                    xx[:, c, HALF + t * P:HALF + (t + 1) * P], rw[:, c, :],
                                                    start=(n == 0), stop=(n == 3))
                                    n += 1
                        ins.then_inc(s_lg, 1)
                        for nb, tiles in enumerate(v_banks):
                            wait(pe, s_vout, 3 * b)
                            for j, t in enumerate(tiles):
                                n = 0
                                for c in range(DC):
                                    for xx, w in ((hi, w_hi), (lo, w_hi), (hi, w_lo)):
                                        ins = pe.matmul(ps[:, bank_v[nb], j * D:(j + 1) * D],
                                                        xx[:, c, t * P:(t + 1) * P], w[:, c, 2 * D:3 * D],
                                                        start=(n == 0), stop=(n == 5))
                                        n += 1
                            ins.then_inc(s_v, 1)


def route(nc, g):
    with ExitStack() as ctx:
        def sb(name, shape, dt=F32):
            return ctx.enter_context(nc.sbuf_tensor(name, shape, dt))

        by = {"sp": [], "pool": [], "v": [], "act": [], "pe": []}

        def sem(name, engine):
            by[engine].append(ctx.enter_context(nc.semaphore(name)))
            return by[engine][-1]

        ps = ctx.enter_context(nc.psum_tensor("ps_route", [P, 4, 512], F32))
        before = sb("before", [P, P])
        ones = sb("ones", [P, P])
        expert_rank = sb("expert_rank", [P, E])
        step_iota = sb("step_iota", [P, STEPS])
        lane_iota = sb("lane_iota", [P, P], BF16)
        half_iota = sb("half_iota", [P, HT], BF16)
        lane = sb("lane", [P, 1])
        top = sb("top", [P, 2, NT])
        pick = sb("pick", [P, 2, NT, E])
        rest = sb("rest", [P, NT, E])
        tied = sb("tied", [P, NT, E])
        win = sb("win", [P, NT])
        both = sb("both", [P, NT, E])
        in_tile = sb("in_tile", [P, NT, E])
        count = sb("count", [P, E, NT])
        through = sb("through", [P, E, NT])
        place = sb("place", [P, NT, E])
        total_i = sb("total_i", [P, E], I32)
        steps_i = sb("steps_i", [P, E], I32)
        steps = sb("steps", [P, E])
        steps_end = sb("steps_end", [P, E])
        first_row = sb("first_row", [P, E])
        passed = sb("passed", [P, STEPS, E])
        expert_f = sb("expert_f", [P, STEPS])
        row = sb("row", [P, 2, NT])
        part_i = sb("part_i", [P, 2, 2, NT], I32)
        part = sb("part", [P, 2, 2, NT])
        ring = 4
        oh_lane = sb("oh_lane", [P, ring, P], BF16)
        oh_half = sb("oh_half", [P, ring, 2, HT], BF16)
        ratio = sb("ratio", [P, NT])
        denom = sb("denom", [P, NT])
        token_f = sb("token_f", [P, HT])

        s_c = sem("s_c", "pool")
        s_v = sem("s_v2", "v")
        s_pick = sem("s_pick", "v")
        s_count = sem("s_count", "pe")
        s_gap = sem("s_gap", "v")
        s_exp = sem("s_exp", "act")
        s_oh = sem("s_oh", "v")
        s_ohmm = sem("s_ohmm", "pe")

        with nc.Block() as block:
            @block.gpsimd
            def _(pool):
                start(pool, by["pool"])
                pool.memset(ones[:], 1.0).then_inc(s_c, 1)
                pool.memset(before[:], 1.0).then_inc(s_c, 1)
                pool.iota(expert_rank[:], [[-1, E]], base=E, channel_multiplier=0,
                          allow_small_or_imprecise_dtypes=True).then_inc(s_c, 1)
                pool.iota(step_iota[:], [[1, STEPS]], base=0, channel_multiplier=0,
                          allow_small_or_imprecise_dtypes=True).then_inc(s_c, 1)
                pool.iota(lane_iota[:], [[1, P]], base=0, channel_multiplier=0,
                          allow_small_or_imprecise_dtypes=True).then_inc(s_c, 1)
                pool.iota(half_iota[:], [[1, HT]], base=0, channel_multiplier=0,
                          allow_small_or_imprecise_dtypes=True).then_inc(s_c, 1)
                pool.iota(lane[:], [[0, 1]], base=0, channel_multiplier=1,
                          allow_small_or_imprecise_dtypes=True).then_inc(s_c, 1)
                wait(pool, s_c, 2)
                pool.affine_select(out=before[:], in_=before[:], compare_op=ALU.is_gt, fill=0.0, base=0,
                                   pattern=[[1, P]], channel_multiplier=-1).then_inc(s_c, 1)

            @block.vector
            def _(v):
                start(v, by["v"])
                chain = Chain(v, s_v)

                def do(ins):
                    chain.add(ins).wait()

                def per_tile(a):
                    return a.unsqueeze(2).to_broadcast([P, NT, E])

                wait(v, s_c, 8)
                rank = expert_rank[:].unsqueeze(1).to_broadcast([P, NT, E])
                for n in range(2):
                    left = g.logits[:] if n == 0 else rest[:]
                    do(v.tensor_reduce(top[:, n, :], left, AX, ALU.max))
                    do(v.tensor_tensor(tied[:], left, per_tile(top[:, n, :]), ALU.is_equal))
                    do(v.tensor_tensor(tied[:], tied[:], rank, ALU.mult))
                    do(v.tensor_reduce(win[:], tied[:], AX, ALU.max))
                    do(v.tensor_tensor(pick[:, n], rank, per_tile(win[:]), ALU.is_equal))
                    if n == 0:
                        do(v.scalar_tensor_tensor(out=rest[:], in0=pick[:, 0], scalar=-FAR, in1=left,
                                                  op0=ALU.mult, op1=ALU.add))
                v.tensor_tensor(ratio[:], top[:, 1, :], top[:, 0, :], ALU.subtract).then_inc(s_gap, 1)
                v.tensor_tensor(both[:], pick[:, 0], pick[:, 1], ALU.add).then_inc(s_pick, 1)
                wait(v, s_exp, 1)
                do(v.tensor_scalar(denom[:], ratio[:], 1.0, None, ALU.add))
                do(v.reciprocal(g.gate[:, 0, :], denom[:]))
                do(v.tensor_tensor(g.gate[:, 1, :], ratio[:], g.gate[:, 0, :], ALU.mult))
                wait(v, s_count, 2)
                v.tensor_copy(in_tile[:], ps[:, 0, 0:NT * E].rearrange("p (t e) -> p t e", e=E))
                do(v.tensor_copy(count[:], ps[:, 1, 0:NT * E].rearrange("p (t e) -> p e t", e=E)))
                for e in range(E):
                    ins = v.tensor_tensor_scan(through[:, e, :], ones[:, 0:NT], count[:, e, :], 0.0,
                                               ALU.mult, ALU.add)
                do(ins)
                do(v.tensor_scalar(total_i[:], through[:, :, NT - 1], float(ROWS - 1), None, ALU.add))
                do(v.tensor_scalar(steps_i[:], total_i[:], ROWS.bit_length() - 1, None,
                                   ALU.arith_shift_right))
                do(v.tensor_copy(steps[:], steps_i[:]))
                do(v.tensor_tensor_scan(steps_end[:], ones[:, 0:E], steps[:], 0.0, ALU.mult, ALU.add))
                do(v.tensor_tensor(first_row[:], steps_end[:], steps[:], ALU.subtract))
                do(v.tensor_scalar(first_row[:], first_row[:], float(ROWS), None, ALU.mult))
                do(v.tensor_tensor(through[:], through[:], count[:], ALU.subtract))
                do(v.tensor_tensor(place[:], in_tile[:], through[:].rearrange("p e t -> p t e"), ALU.add))
                do(v.tensor_tensor(place[:], place[:], first_row[:].unsqueeze(1).to_broadcast([P, NT, E]),
                                   ALU.add))
                do(v.tensor_tensor(passed[:], step_iota[:].unsqueeze(2).to_broadcast([P, STEPS, E]),
                                   steps_end[:].unsqueeze(1).to_broadcast([P, STEPS, E]), ALU.is_ge))
                do(v.tensor_reduce(expert_f[:], passed[:], AX, ALU.add))
                do(v.tensor_scalar(g.step_expert[:], expert_f[:], float(E - 1), None, ALU.min))
                for n in range(2):
                    do(v.tensor_tensor(rest[:], pick[:, n], place[:], ALU.mult))
                    do(v.tensor_reduce(row[:, n, :], rest[:], AX, ALU.add))
                do(v.tensor_copy(g.token_row[:], row[:]))
                v.tensor_scalar(part_i[:, 0], g.token_row[:], P.bit_length() - 1, None, ALU.arith_shift_right)
                do(v.tensor_scalar(part_i[:, 1], g.token_row[:], P - 1, None, ALU.bitwise_and))
                do(v.tensor_copy(part[:], part_i[:]))
                for n in range(2):
                    for t in range(NT):
                        at = n * NT + t
                        if at >= ring:
                            wait(v, s_ohmm, at - ring + 1)
                        half = part[:, 0, n, t:t + 1]
                        v.tensor_scalar(oh_lane[:, at % ring], lane_iota[:], part[:, 1, n, t:t + 1], None,
                                        ALU.is_equal)
                        v.tensor_scalar(oh_half[:, at % ring, 0], half_iota[:], half, float(t),
                                        ALU.is_equal, ALU.mult)
                        v.tensor_scalar(oh_half[:, at % ring, 1], half_iota[:], half, lane[:],
                                        ALU.is_equal, ALU.mult).then_inc(s_oh, 1)
                wait(v, s_ohmm, 2 * NT)
                do(v.tensor_copy(token_f[:], ps[:, 2, HT:2 * HT]))
                do(v.scalar_tensor_tensor(out=g.row_token[:], in0=ps[:, 2, 0:HT], scalar=float(P),
                                          in1=token_f[:], op0=ALU.mult, op1=ALU.add))

            @block.scalar
            def _(act):
                start(act, by["act"])
                wait(act, s_gap, 1)
                act.activation(ratio[:], ratio[:], ACT.Exp).then_inc(s_exp, 1)

            @block.tensor
            def _(pe):
                start(pe, by["pe"])
                wait(pe, s_c, 8)
                wait(pe, s_pick, 1)
                sel = both[:].rearrange("p t e -> p (t e)")
                pe.matmul(ps[:, 0, 0:NT * E], before[:], sel, start=True, stop=True).then_inc(s_count, 1)
                pe.matmul(ps[:, 1, 0:NT * E], ones[:], sel, start=True, stop=True).then_inc(s_count, 1)
                for at in range(2 * NT):
                    wait(pe, s_oh, at + 1)
                    pe.matmul(ps[:, 2, 0:2 * HT], oh_lane[:, at % ring],
                              oh_half[:, at % ring].rearrange("p a h -> p (a h)"),
                              start=(at == 0), stop=(at == 2 * NT - 1)).then_inc(s_ohmm, 1)


def attend(nc, g):
    with ExitStack() as ctx:
        def sb(name, shape, dt=F32):
            return ctx.enter_context(nc.sbuf_tensor(name, shape, dt))

        by = {"sp": [], "pool": [], "v": [], "act": [], "pe": []}

        def sem(name, engine):
            by[engine].append(ctx.enter_context(nc.semaphore(name)))
            return by[engine][-1]

        W = 2 * P
        ps = ctx.enter_context(nc.psum_tensor("ps_attend", [P, 8, 512], F32))
        wo_raw = sb("wo_raw", [P, DC, D])
        wo_hi = sb("wo_hi", [P, DC, D], F32R)
        wo_lo = sb("wo_lo", [P, DC, D], F32R)
        b_o = sb("b_o", [P, D])
        band = sb("band", [P, W])
        head_rows = sb("head_rows", [P, HC])
        q_s = sb("q_s", [P, 2, N], F32R)
        k_s = sb("k_s", [P, 2, 2, N], F32R)
        v_s = sb("v_s", [P, 2, VT, P], F32R)
        q_m = sb("q_m", [P, 2, 2, N], F32R)
        v_m = sb("v_m", [P, 2, 2, VT, P], F32R)
        wt = sb("wt", [P, 2, TB, W])
        low = sb("low", [P, 2, TB])
        total = sb("total", [P, DC, TB, HC])
        inv = sb("inv", [P, TB, HC, DH])
        inv_t = sb("inv_t", [P, N])
        pt_hi = sb("pt_hi", [P, 2, 512], F32R)
        pt_lo = sb("pt_lo", [P, 2, 512], F32R)
        a_hi = sb("a_hi", [P, DC, N], F32R)
        a_lo = sb("a_lo", [P, DC, N], F32R)
        xb = sb("xb", [P, TB, D])

        s_in = sem("s_in", "sp")
        s_const = sem("s_const", "pool")
        s_wohi = sem("s_wohi", "act")
        s_wolo = sem("s_wolo", "v")
        s_xb = sem("s_xb", "sp")
        s_out = sem("s_out", "sp")
        s_wload = sem("s_wload", "sp")
        s_hi = sem("s_hi3", "act")
        s_lo = sem("s_lo3", "v")
        s_vhi = sem("s_vhi", "act")
        s_vlo = sem("s_vlo", "v")
        s_qm = sem("s_qm", "v")
        s_vz = sem("s_vz", "pool")
        s_vm = sem("s_vm", "pool")
        s_s = sem("s_s", "pe")
        s_low = sem("s_low", "v")
        s_exp = sem("s_exp3", "act")
        s_t = sem("s_t", "pe")
        s_phi = sem("s_phi", "act")
        s_plo = sem("s_plo", "v")
        s_pv = sem("s_pv", "pe")
        s_inv = sem("s_inv", "v")
        s_invt = sem("s_invt", "pe")
        s_invs = sem("s_invs", "act")
        s_a = sem("s_a", "v")
        s_ahi = sem("s_ahi", "act")
        s_alo = sem("s_alo", "v")
        s_proj = sem("s_proj", "pe")
        s_done = sem("s_done", "v")
        s_dve = sem("s_dve3", "v")

        bank_s, bank_t, bank_o, bank_m = ((0, 1), (2, 3)), (4, 5), 6, 7
        heads = DC * HC
        x_rows = g.x.rearrange("b (t p) d -> b p t d", p=P)
        base_rows = g.base_dram.rearrange("(b t p) d -> b p t d", t=TB, p=P)

        def window(i):
            first = max(0, HALF - P * i)
            last = min(W, N + HALF - P * i)
            return first, last, first + P * i - HALF

        with nc.Block() as block:
            @block.sync
            def _(sp):
                start(sp, by["sp"])
                sp.dma_start(wo_raw[:], g.Wout.rearrange("(c p) n -> p c n", p=P)).then_inc(s_in, 16)
                sp.dma_start(b_o[:], g.bout.partition_broadcast(P)).then_inc(s_in, 16)
                with sp.Fori(0, B) as b:
                    wait_first(sp, s_out, 16 * b, g.tick)
                    sp.dma_start(xb[:], x_rows[ds(b, 1)].rearrange("b p t d -> (b p) t d")).then_inc(s_xb, 16)
                    wait_first(sp, s_done, 2 * b + 2, g.tick)
                    sp.dma_start(base_rows[ds(b, 1)].rearrange("b p t d -> (b p) t d"), xb[:]).then_inc(s_out, 16)
                    wait_first(sp, s_wload, 32 * b, g.tick)
                    sp.dma_start(g.w1_of(b), g.w1[ds(b, 1)].rearrange("e (c p) f -> (e p) c f", p=P)).then_inc(s_wload, 16)
                    sp.dma_start(g.w2_of(b), g.w2[ds(b, 1)].rearrange("e (m p) d -> (e p) m d", p=P)).then_inc(s_wload, 16)
                wait(sp, s_out, 16 * B)
                wait(sp, s_wload, 32 * E)

            @block.gpsimd
            def _(pool):
                start(pool, by["pool"])
                pool.memset(band[:], 0.0).then_inc(s_vz, 1)
                pool.memset(head_rows[:], 1.0).then_inc(s_vz, 1)
                wait(pool, s_vz, 2)
                pool.affine_select(out=band[:], in_=band[:], compare_op=ALU.is_ge, fill=FAR, base=0,
                                   pattern=[[1, W]], channel_multiplier=-1).then_inc(s_vz, 1)
                pool.affine_select(out=head_rows[:], in_=head_rows[:], compare_op=ALU.is_ge, fill=0.0,
                                   base=0, pattern=[[-DH, HC]], channel_multiplier=1).then_inc(s_vz, 1)
                wait(pool, s_vz, 4)
                pool.affine_select(out=band[:], in_=band[:], compare_op=ALU.is_ge, fill=FAR, base=2 * HALF,
                                   pattern=[[-1, W]], channel_multiplier=1).then_inc(s_const, 1)
                pool.affine_select(out=head_rows[:], in_=head_rows[:], compare_op=ALU.is_ge, fill=0.0,
                                   base=DH - 1, pattern=[[DH, HC]], channel_multiplier=-1).then_inc(s_const, 1)
                for ring in range(2):
                    pool.memset(v_m[:, ring].bitcast(F32), 0.0).then_inc(s_const, 1)
                pool.memset(wt[:, :, 0, 0:HALF], 0.0).then_inc(s_const, 1)
                pool.memset(wt[:, :, TB - 1, W - HALF:W], 0.0).then_inc(s_const, 1)
                wait(pool, s_const, 6)
                with pool.Fori(0, B) as b:
                    for n in range(heads):
                        c, j, ring = n // HC, n % HC, n % 2
                        m = heads * b + n
                        if j == 0:
                            wait_first(pool, s_vlo, 2 * b + c + 1, g.tick)
                        wait_first(pool, s_pv, m + 1, g.tick)
                        old = DH * ((j - 2) % HC)
                        pool.memset(v_m[:, ring, :, :, old:old + DH].rearrange("p h t d -> p (h t) d").bitcast(F32), 0.0)
                        pool.tensor_copy(v_m[:, ring, :, :, DH * j:DH * (j + 1)].rearrange("p h t d -> p (h t) d"),
                                         v_s[:, :, :, DH * j:DH * (j + 1)].rearrange("p h t d -> p (h t) d")).then_inc(s_vm, 1)

            @block.vector
            def _(v):
                start(v, by["v"])
                wait(v, s_wohi, 1)
                v.tensor_tensor(wo_lo[:], wo_raw[:], wo_hi[:].bitcast(F32), ALU.subtract).then_inc(s_wolo, 1)
                v.sem_inc(s_low, 2)
                v.sem_inc(s_plo, 2)
                wait(v, s_const, 6)
                with v.Fori(0, B) as b:
                    def lo_of_chunk(c):
                        wait(v, s_hi, 2 * b + c + 1)
                        q, k = g.q_of(b, c), g.k_of(b, c)
                        v.scalar_tensor_tensor(out=q_s[:, 1], in0=q, scalar=-DH ** -0.5,
                                               in1=q_s[:, 0].bitcast(F32), op0=ALU.mult, op1=ALU.subtract)
                        v.tensor_tensor(k_s[:, c, 1], k, k_s[:, c, 0].bitcast(F32), ALU.subtract
                                        ).then_inc(s_lo, 1)

                    def lo_of_values(c):
                        wait(v, s_vhi, 2 * b + c + 1)
                        v.tensor_tensor(v_s[:, 1], g.v_chunk(b, c), v_s[:, 0].bitcast(F32), ALU.subtract
                                        ).then_inc(s_vlo, 1)

                    def one_head(n):
                        m, j, ring = heads * b + n, n % HC, n % 2
                        wait(v, s_s, m + 1)
                        if j == 0:
                            wait(v, s_lo, 2 * b + n // HC + 1)
                        v.tensor_scalar(q_m[:, ring], q_s[:].bitcast(F32), head_rows[:, j:j + 1], None,
                                        ALU.mult).then_inc(s_qm, 1)

                    def mask(n):
                        m, ring = heads * b + n, n % 2
                        wait(v, s_s, m + 3)
                        wait_first(v, s_t, 2 * m - 2 if n > 1 else 2 * heads * b, g.tick)
                        for i in range(TB):
                            f, l, _ = window(i)
                            bank = bank_s[ring][i // 2]
                            ins = v.tensor_tensor_reduce(
                                out=wt[:, ring, i, f:l], in0=ps[:, bank, W * (i % 2) + f:W * (i % 2) + l],
                                in1=band[:, f:l], scale=1.0, scalar=FAR, op0=ALU.add, op1=ALU.min,
                                accum_out=low[:, ring, i:i + 1])
                        ins.then_inc(s_low, 1)

                    def lo_of_weights(n):
                        m = heads * b + n
                        for h in range(2):
                            wait(v, s_phi, 2 * m + h + 1)
                            v.tensor_tensor(pt_lo[:, h, :], ps[:, bank_t[h], :], pt_hi[:, h, :].bitcast(F32),
                                            ALU.subtract).then_inc(s_plo, 1)

                    def normalise(c):
                        u = 2 * b + c
                        wait(v, s_pv, heads * b + HC * (c + 1) + 2)
                        wait(v, s_invs, u + 1)
                        v.tensor_tensor(inv_t[:], ps[:, bank_o, :], inv_t[:], ALU.mult).then_inc(s_a, 1)
                        wait(v, s_ahi, u + 1)
                        v.tensor_tensor(a_lo[:, c], inv_t[:], a_hi[:, c].bitcast(F32), ALU.subtract).then_inc(s_alo, 1)

                    def invert(c):
                        wait(v, s_exp, heads * b + HC * (c + 1))
                        v.reciprocal(inv[:], total[:, c].unsqueeze(3).to_broadcast([P, TB, HC, DH])).then_inc(s_inv, 1)

                    lo_of_chunk(0)
                    one_head(0)
                    one_head(1)
                    mask(0)
                    mask(1)
                    lo_of_values(0)
                    wait(v, s_xb, 16 * b + 16)
                    v.tensor_tensor(xb[:], xb[:], b_o[:].unsqueeze(1).to_broadcast([P, TB, D]), ALU.add).then_inc(s_dve, 1)
                    for n in range(heads):
                        if n + 2 < heads:
                            one_head(n + 2)
                        lo_of_weights(n)
                        if n == HC - 1:
                            invert(0)
                        if n == HC:
                            normalise(0)
                        if n == HC - 3:
                            lo_of_chunk(1)
                        if n == HC - 1:
                            lo_of_values(1)
                        if n + 2 < heads:
                            mask(n + 2)
                    invert(1)
                    normalise(1)
                    wait(v, s_dve, b + 1)
                    for h in range(2):
                        wait(v, s_proj, 2 * b + h + 1)
                        v.tensor_tensor(xb[:, 2 * h:2 * h + 2], ps[:, bank_m, :].rearrange("p (t d) -> p t d", d=D),
                                        xb[:, 2 * h:2 * h + 2], ALU.add).then_inc(s_done, 1)

            @block.scalar
            def _(act):
                start(act, by["act"])
                wait(act, s_in, 32)
                act.activation(wo_hi[:], wo_raw[:], ACT.Copy).then_inc(s_wohi, 1)
                wait(act, s_const, 6)
                with act.Fori(0, B) as b:
                    def hi_of_chunk(c):
                        q, k = g.q_of(b, c), g.k_of(b, c)
                        act.activation(q_s[:, 0], q, ACT.Copy, scale=-DH ** -0.5)
                        act.activation(k_s[:, c, 0], k, ACT.Copy).then_inc(s_hi, 1)

                    def hi_of_values(c):
                        wait(act, s_vm, heads * b + HC * c)
                        act.activation(v_s[:, 0], g.v_chunk(b, c), ACT.Copy).then_inc(s_vhi, 1)

                    def exponentials(n):
                        m, c, j, ring = heads * b + n, n // HC, n % HC, n % 2
                        if j == 0:
                            wait(act, s_inv, 2 * b)
                        wait(act, s_low, m + 3)
                        for i in range(TB):
                            f, l, _ = window(i)
                            ins = act.activation(wt[:, ring, i, f:l], wt[:, ring, i, f:l], ACT.Exp,
                                                 bias=low[:, ring, i:i + 1], scale=-1.0,
                                                 accum_out=total[:, c, i, j:j + 1])
                        ins.then_inc(s_exp, 1)

                    def hi_of_weights(n):
                        m = heads * b + n
                        wait(act, s_pv, m + 2)
                        for h in range(2):
                            wait(act, s_t, 2 * m + h + 1)
                            act.activation(pt_hi[:, h, :], ps[:, bank_t[h], :], ACT.Copy).then_inc(s_phi, 1)

                    def out_of_chunk(c):
                        u = 2 * b + c
                        wait(act, s_invt, u + 1)
                        wait(act, s_alo, u)
                        act.activation(inv_t[:], ps[:, bank_m, :], ACT.Copy).then_inc(s_invs, 1)
                        wait(act, s_a, u + 1)
                        wait(act, s_proj, 2 * b)
                        act.activation(a_hi[:, c], inv_t[:], ACT.Copy).then_inc(s_ahi, 1)

                    wait(act, s_s, heads * b + 2)
                    hi_of_chunk(0)
                    hi_of_values(0)
                    exponentials(0)
                    exponentials(1)
                    for n in range(heads):
                        hi_of_weights(n)
                        if n == HC:
                            out_of_chunk(0)
                        if n == HC - 3:
                            wait(act, s_qm, heads * b + HC)
                            hi_of_chunk(1)
                        if n == HC - 1:
                            hi_of_values(1)
                        if n + 2 < heads:
                            exponentials(n + 2)
                    out_of_chunk(1)

            @block.tensor
            def _(pe):
                start(pe, by["pe"])
                pe.sem_inc(s_s, 2)
                pe.sem_inc(s_pv, 2)
                wait(pe, s_wolo, 1)
                wait(pe, s_const, 6)
                with pe.Fori(0, B) as b:
                    def scores(n):
                        m, c, ring = heads * b + n, n // HC, n % 2
                        wait(pe, s_qm, m + 1)
                        wait(pe, s_low, m + 1)
                        if n % HC == 0:
                            wait(pe, s_lo, 2 * b + c + 1)
                        for i in range(TB):
                            f, l, key = window(i)
                            for p, (a, k) in enumerate(((0, 0), (0, 1), (1, 0))):
                                ins = pe.matmul(ps[:, bank_s[ring][i // 2], W * (i % 2) + f:W * (i % 2) + l],
                                                q_m[:, ring, a, i * P:(i + 1) * P],
                                                k_s[:, c, k, key:key + l - f], start=(p == 0), stop=(p == 2))
                        ins.then_inc(s_s, 1)

                    def transposes(n):
                        m, ring = heads * b + n, n % 2
                        wait(pe, s_exp, m + 1)
                        for i in range(TB):
                            if i % 2 == 0:
                                wait(pe, s_plo, 2 * m + i // 2 + 1)
                            for h in range(2):
                                at = (2 * i + h) % TB
                                ins = pe.transpose(ps[:, bank_t[i // 2], at * P:(at + 1) * P],
                                                   wt[:, ring, i, h * P:(h + 1) * P], g.ident[:])
                            if i % 2:
                                ins.then_inc(s_t, 1)

                    def weighted_values(n):
                        m, c, j, ring = heads * b + n, n // HC, n % HC, n % 2
                        wait(pe, s_vm, m + 1)
                        wait(pe, s_plo, 2 * m + 4)
                        if j == 0:
                            wait(pe, s_a, 2 * b + c)
                        hi = pt_hi[:].rearrange("p h n -> p (h n)")
                        lo = pt_lo[:].rearrange("p h n -> p (h n)")
                        for t in range(VT):
                            a, z = max(0, (2 * t - 1) * P), min(2 * N, (2 * t + 1) * P)
                            o = max(0, (t - 1) * P)
                            for p, (vv, w) in enumerate(((0, hi), (0, lo), (1, hi))):
                                ins = pe.matmul(ps[:, bank_o, o:o + z - a], v_m[:, ring, vv, t, :], w[:, a:z],
                                                start=(j == 0 and t == 0 and p == 0),
                                                stop=(j == HC - 1 and t == VT - 1 and p == 2),
                                                skip_group_check=True)
                        ins.then_inc(s_pv, 1)

                    def transpose_inverse(c):
                        wait(pe, s_inv, 2 * b + c + 1)
                        wait(pe, s_done, 2 * b)
                        for i in range(TB):
                            ins = pe.transpose(ps[:, bank_m, i * P:(i + 1) * P],
                                               inv[:, i].rearrange("p h d -> p (h d)"), g.ident[:])
                        ins.then_inc(s_invt, 1)

                    scores(0)
                    scores(1)
                    for n in range(heads):
                        transposes(n)
                        if n == HC:
                            transpose_inverse(0)
                        if n:
                            weighted_values(n - 1)
                        if n + 2 < heads:
                            scores(n + 2)
                    transpose_inverse(1)
                    weighted_values(heads - 1)
                    wait(pe, s_alo, 2 * b + 2)
                    for h in range(2):
                        wait(pe, s_done, 2 * b + h)
                        for t in range(2):
                            k = 0
                            tok = (2 * h + t) * P
                            for c in range(DC):
                                for a, w in ((a_hi, wo_hi), (a_lo, wo_hi), (a_hi, wo_lo)):
                                    ins = pe.matmul(ps[:, bank_m, t * D:(t + 1) * D], a[:, c, tok:tok + P],
                                                    w[:, c, :], start=(k == 0), stop=(k == 5))
                                    k += 1
                        ins.then_inc(s_proj, 1)


def experts(nc, g):
    with ExitStack() as ctx:
        def sb(name, shape, dt=F32):
            return ctx.enter_context(nc.sbuf_tensor(name, shape, dt))

        by = {"sp": [], "pool": [], "v": [], "act": [], "pe": []}

        def sem(name, engine):
            by[engine].append(ctx.enter_context(nc.semaphore(name)))
            return by[engine][-1]

        def dma_sem(name):
            return ctx.enter_context(nc.semaphore(name))

        ps = ctx.enter_context(nc.psum_tensor("ps_experts", [P, 8, 512], F32))
        w1_hi = sb("w1_hi", [P, DC, F], F32R)
        w1_lo = sb("w1_lo", [P, DC, F], F32R)
        w2_hi = sb("w2_hi", [P, FC, D], F32R)
        w2_lo = sb("w2_lo", [P, FC, D], F32R)
        b1 = sb("b1_s", [P, E * FC])
        b2 = sb("b2_s", [P, E, D])
        index = sb("index", [P, 2, 2], U32)
        xg = sb("xg", [P, 2, 2, D])
        xt_hi = sb("xgt_hi", [P, DC, ROWS], F32R)
        xt_lo = sb("xgt_lo", [P, DC, ROWS], F32R)
        hid = sb("hid", [P, 2, 2, ROWS])
        h_hi = sb("h_hi", [P, FC, ROWS], F32R)
        h_lo = sb("h_lo", [P, FC, ROWS], F32R)
        y = sb("y", [P, 2, 2, D])

        s_in = sem("s_in4", "sp")
        s_idx = sem("s_idx", "pool")
        s_g = [dma_sem("s_g0"), dma_sem("s_g1")]
        s_tr = sem("s_tr4", "pe")
        s_xhi = sem("s_xhi", "act")
        s_xlo = sem("s_xlo", "v")
        s_w1hi = sem("s_w1hi", "act")
        s_w1lo = sem("s_w1lo", "v")
        s_w2hi = sem("s_w2hi", "act")
        s_w2lo = sem("s_w2lo", "v")
        s_l1 = sem("s_l1", "pe")
        s_hid = sem("s_hid", "act")
        s_hhi = sem("s_hhi", "v")
        s_h = sem("s_h", "v")
        s_l2 = sem("s_l2", "pe")
        s_y = sem("s_y", "v")
        s_yout = sem("s_yout", "sp")

        bank_h, bank_t, bank_y = (0, 1, 2, 3), 4, (5, 6)
        FG, MG = F // 2, FC // 2
        y_rows = g.y_dram.rearrange("(s h p) d -> s p h d", h=2, p=P)

        def expert_of(eng, s):
            return eng.value_load(g.step_expert[0:1, ds(s, 1)], min_val=0, max_val=E - 1)

        with nc.Block() as block:
            @block.sync
            def _(sp):
                start(sp, by["sp"])
                sp.dma_start(b1[:], g.b1_cols).then_inc(s_in, 16)
                sp.dma_start(b2[:], g.b2.partition_broadcast(P)).then_inc(s_in, 16)
                with sp.Fori(0, STEPS // 2) as pair:
                    for par in range(2):
                        s = 2 * pair + par
                        wait_first(sp, s_yout, 16 * s, g.tick)
                        wait_first(sp, s_y, s + 1, g.tick)
                        sp.dma_start(y_rows[ds(s, 1)].rearrange("s p h d -> (s p) h d"), y[:, par]
                                     ).then_inc(s_yout, 16)
                wait(sp, s_yout, 16 * STEPS)

            @block.gpsimd
            def _(pool):
                start(pool, by["pool"])
                def gather(s, row_step, ring):
                    pool.tensor_copy(index[:, ring], g.row_token[:, ds(2 * row_step, 2)]).then_inc(s_idx, 1)
                    wait_first(pool, s_idx, s + 1, g.tick)
                    for h in range(2):
                        pool.indirect_dma_start(
                            xg[:, ring, h], None, g.xn_dram,
                            bass.IndirectOffsetOnAxis(ap=index[:, ring, h:h + 1], axis=0)
                            ).then_inc(s_g[h], 16)

                gather(0, 0, 0)
                with pool.Fori(0, STEPS // 2) as pair:
                    for par in range(2):
                        s = 2 * pair + par
                        for h in range(2):
                            pool.wait_ge(s_g[h], 16 * s + 16)
                            pool.sem_inc(g.tick, 1)
                        wait_first(pool, s_tr, s, g.tick)
                        gather(s + 1, (s + 1) % STEPS, 1 - par)
                for h in range(2):
                    pool.wait_ge(s_g[h], 16 * (STEPS + 1))

            @block.vector
            def _(v):
                start(v, by["v"])
                def lo_of_w1(s, e, n):
                    wait(v, s_w1hi, 2 * s + n + 1)
                    cols = slice(n * FG, (n + 1) * FG)
                    v.tensor_tensor(w1_lo[:, :, cols], g.w1_of(e)[:, :, cols], w1_hi[:, :, cols].bitcast(F32),
                                    ALU.subtract).then_inc(s_w1lo, 1)

                def lo_of_w2(s, e, n):
                    wait(v, s_w2hi, 2 * s + n + 1)
                    m = slice(n * MG, (n + 1) * MG)
                    v.tensor_tensor(w2_lo[:, m], g.w2_of(e)[:, m], w2_hi[:, m].bitcast(F32),
                                    ALU.subtract).then_inc(s_w2lo, 1)

                def lo_of_rows(s):
                    wait(v, s_xhi, s + 1)
                    v.tensor_tensor(xt_lo[:].rearrange("p c n -> p (c n)"), ps[:, bank_t, :],
                                    xt_hi[:].rearrange("p c n -> p (c n)").bitcast(F32),
                                    ALU.subtract).then_inc(s_xlo, 1)

                def hidden(s, n):
                    wait(v, s_hid, 4 * s + n + 1)
                    v.tensor_copy(h_hi[:, 2 * n:2 * n + 2], hid[:, n % 2]).then_inc(s_hhi, 1)
                    wait(v, s_hhi, 4 * s + n + 1)
                    v.tensor_tensor(h_lo[:, 2 * n:2 * n + 2], hid[:, n % 2],
                                    h_hi[:, 2 * n:2 * n + 2].bitcast(F32), ALU.subtract).then_inc(s_h, 1)

                wait(v, s_in, 32)
                first = expert_of(v, 0)
                lo_of_w1(0, first, 0)
                lo_of_rows(0)
                lo_of_w1(0, first, 1)
                lo_of_w2(0, first, 0)
                with v.Fori(0, STEPS // 2) as pair:
                    for par in range(2):
                        s = 2 * pair + par
                        e, e_next = expert_of(v, s), expert_of(v, (s + 1) % STEPS)
                        hidden(s, 0)
                        hidden(s, 1)
                        lo_of_w2(s, e, 1)
                        hidden(s, 2)
                        hidden(s, 3)
                        lo_of_w1(s + 1, e_next, 0)
                        lo_of_rows(s + 1)
                        lo_of_w1(s + 1, e_next, 1)
                        lo_of_w2(s + 1, e_next, 0)
                        wait(v, s_l2, 2 * s + 2)
                        wait(v, s_yout, 16 * s)
                        v.tensor_tensor(y[:, par], ps[:, bank_y[0]:bank_y[1] + 1, 0:D],
                                        b2[:, ds(e, 1), :].to_broadcast([P, 2, D]), ALU.add).then_inc(s_y, 1)

            @block.scalar
            def _(act):
                start(act, by["act"])
                def hi_of_w1(e, n):
                    cols = slice(n * FG, (n + 1) * FG)
                    act.activation(w1_hi[:, :, cols], g.w1_of(e)[:, :, cols], ACT.Copy).then_inc(s_w1hi, 1)

                def hi_of_w2(e, n):
                    m = slice(n * MG, (n + 1) * MG)
                    act.activation(w2_hi[:, m], g.w2_of(e)[:, m], ACT.Copy).then_inc(s_w2hi, 1)

                def hi_of_rows(s):
                    wait_first(act, s_tr, s + 1, g.tick)
                    act.activation(xt_hi[:].rearrange("p c n -> p (c n)"), ps[:, bank_t, :], ACT.Copy
                                   ).then_inc(s_xhi, 1)

                def hidden(s, e, n):
                    wait_first(act, s_l1, 4 * s + n + 1, g.tick)
                    wait_first(act, s_h, 4 * s + n - 1 if n > 1 else 4 * s, g.tick)
                    for j in range(2):
                        ins = act.activation(hid[:, n % 2, j], ps[:, bank_h[n], j * ROWS:(j + 1) * ROWS],
                                             ACT.Relu, bias=b1[:, ds(e * FC + 2 * n + j, 1)])
                    ins.then_inc(s_hid, 1)

                wait(act, s_in, 32)
                first = expert_of(act, 0)
                hi_of_w1(first, 0)
                hi_of_rows(0)
                hi_of_w1(first, 1)
                hi_of_w2(first, 0)
                with act.Fori(0, STEPS // 2) as pair:
                    for par in range(2):
                        s = 2 * pair + par
                        e, e_next = expert_of(act, s), expert_of(act, (s + 1) % STEPS)
                        hidden(s, e, 0)
                        hi_of_w2(e, 1)
                        hidden(s, e, 1)
                        hidden(s, e, 2)
                        hidden(s, e, 3)
                        hi_of_w1(e_next, 0)
                        hi_of_rows(s + 1)
                        hi_of_w1(e_next, 1)
                        wait_first(act, s_l2, 2 * s + 1, g.tick)
                        hi_of_w2(e_next, 0)

            @block.tensor
            def _(pe):
                start(pe, by["pe"])
                def transpose_rows(s, ring):
                    for h in range(2):
                        pe.wait_ge(s_g[h], 16 * s + 16)
                    wait(pe, s_xlo, s)
                    for c in range(DC):
                        for h in range(2):
                            ins = pe.transpose(ps[:, bank_t, (c * 2 + h) * P:(c * 2 + h + 1) * P],
                                               xg[:, ring, h, c * P:(c + 1) * P], g.ident[:])
                    ins.then_inc(s_tr, 1)

                transpose_rows(0, 0)
                with pe.Fori(0, STEPS // 2) as pair:
                    for par in range(2):
                        s = 2 * pair + par
                        wait(pe, s_xlo, s + 1)
                        wait(pe, s_hid, 4 * s)
                        for m in range(FC):
                            if m % MG == 0:
                                wait(pe, s_w1lo, 2 * s + m // MG + 1)
                            k = 0
                            for c in range(DC):
                                for w, xx in ((w1_hi, xt_hi), (w1_hi, xt_lo), (w1_lo, xt_hi)):
                                    ins = pe.matmul(ps[:, bank_h[m // 2], m % 2 * ROWS:(m % 2 + 1) * ROWS],
                                                    w[:, c, m * P:(m + 1) * P], xx[:, c, :],
                                                    start=(k == 0), stop=(k == 5))
                                    k += 1
                            if m % 2:
                                ins.then_inc(s_l1, 1)
                        wait(pe, s_y, s)
                        transpose_rows(s + 1, 1 - par)
                        for m in range(FC):
                            if m % MG == 0:
                                wait(pe, s_w2lo, 2 * s + m // MG + 1)
                            if m % 2 == 0:
                                wait(pe, s_h, 4 * s + m // 2 + 1)
                            for h in range(2):
                                for k, (a, w) in enumerate(((h_hi, w2_hi), (h_lo, w2_hi), (h_hi, w2_lo))):
                                    ins = pe.matmul(ps[:, bank_y[h], 0:D], a[:, m, h * P:(h + 1) * P], w[:, m, :],
                                                    start=(m == 0 and k == 0), stop=(m == FC - 1 and k == 2))
                            if m % MG == MG - 1:
                                ins.then_inc(s_l2, 1)


def combine(nc, g):
    with ExitStack() as ctx:
        def sb(name, shape, dt=F32):
            return ctx.enter_context(nc.sbuf_tensor(name, shape, dt))

        by = {"sp": [], "pool": [], "v": [], "act": [], "pe": []}

        def sem(name, engine):
            by[engine].append(ctx.enter_context(nc.semaphore(name)))
            return by[engine][-1]

        def dma_sem(name):
            return ctx.enter_context(nc.semaphore(name))

        index = sb("index5", [P, 2, 2, TB], U32)
        base = sb("base", [P, 2, TB, D])
        rows = sb("rows", [P, 2, 2, TB, D])
        s_idx = sem("s_idx5", "pool")
        s_base = sem("s_base", "sp")
        s_g = [[dma_sem(f"s_rows{n}{t}") for t in range(TB)] for n in range(2)]
        s_sum = sem("s_sum", "v")
        s_sent = sem("s_sent", "sp")

        base_rows = g.base_dram.rearrange("(b t p) d -> b p t d", t=TB, p=P)
        out_rows = g.out.rearrange("b (t p) d -> b p t d", p=P)

        with nc.Block() as block:
            @block.sync
            def _(sp):
                start(sp, by["sp"])
                def load(b, par):
                    sp.dma_start(base[:, par], base_rows[ds(b, 1)].rearrange("b p t d -> (b p) t d")
                                 ).then_inc(s_base, 16)

                load(0, 0)
                with sp.Fori(0, B // 2) as pair:
                    for par in range(2):
                        b = 2 * pair + par
                        following = (b + 1) % B
                        wait_first(sp, s_base, 16 * b + 16, g.tick)
                        wait_first(sp, s_sent, 16 * b, g.tick)
                        load(following, 1 - par)
                        wait_first(sp, s_sum, 4 * b + 4, g.tick)
                        sp.dma_start(out_rows[ds(b, 1)].rearrange("b p t d -> (b p) t d"), base[:, par]
                                     ).then_inc(s_sent, 16)
                wait(sp, s_sent, 16 * B)
                wait(sp, s_base, 16 * (B + 1))

            @block.gpsimd
            def _(pool):
                start(pool, by["pool"])
                def gather(count, b, ring):
                    pool.tensor_copy(index[:, ring], g.token_row[:, :, ds(b * TB, TB)]).then_inc(s_idx, 1)
                    wait_first(pool, s_idx, count, g.tick)
                    for t in range(TB):
                        for n in range(2):
                            pool.indirect_dma_start(
                                rows[:, ring, n, t], None, g.y_dram,
                                bass.IndirectOffsetOnAxis(ap=index[:, ring, n, t:t + 1], axis=0)
                                ).then_inc(s_g[n][t], 16)

                gather(1, 0, 0)
                with pool.Fori(0, B // 2) as pair:
                    for par in range(2):
                        b = 2 * pair + par
                        for n in range(2):
                            for t in range(TB):
                                pool.wait_ge(s_g[n][t], 16 * b + 16)
                                pool.sem_inc(g.tick, 1)
                        wait_first(pool, s_sum, 4 * b, g.tick)
                        gather(b + 2, (b + 1) % B, 1 - par)
                for n in range(2):
                    for t in range(TB):
                        pool.wait_ge(s_g[n][t], 16 * (B + 1))

            @block.vector
            def _(v):
                start(v, by["v"])
                with v.Fori(0, B // 2) as pair:
                    for par in range(2):
                        b = 2 * pair + par
                        chain = Chain(v, s_sum, 4 * b)
                        for n in range(2):
                            for t in range(TB):
                                v.wait_ge(s_g[n][t], 16 * b + 16)
                            gate = g.gate[:, n, ds(b * TB, TB)].unsqueeze(2).to_broadcast([P, TB, D])
                            chain.add(v.tensor_tensor(rows[:, par, n], rows[:, par, n], gate, ALU.mult))
                        wait(v, s_base, 16 * b + 16)
                        chain.wait()
                        chain.add(v.tensor_tensor(rows[:, par, 0], rows[:, par, 0], rows[:, par, 1], ALU.add)).wait()
                        chain.add(v.tensor_tensor(base[:, par], base[:, par], rows[:, par, 0], ALU.add))


def build(nc, g):
    with ExitStack() as ctx:
        def sb(name, shape, dt=F32):
            return ctx.enter_context(nc.sbuf_tensor(name, shape, dt))

        g.base_dram = nc.dram_tensor("base_rows", (T, D), F32).ap()
        g.xn_dram = nc.dram_tensor("xn_rows", (T, D), F32).ap()
        g.y_dram = nc.dram_tensor("expert_rows", (SLOTS, D), F32).ap()
        per_expert = DC * F + FC * D
        per_batch = 2 * DC * N + VT * D
        g.pool = sb("weights_qkv", [P, E * per_expert])
        start = E * per_expert - B * per_batch
        g.ident = sb("ident", [P, P])
        g.logits = sb("logits", [P, NT, E])
        g.gate = sb("gate", [P, 2, NT])
        g.token_row = sb("token_row", [P, 2, NT], I32)
        g.row_token = sb("row_token", [P, HT], U32)
        g.step_expert = sb("step_expert", [P, STEPS], I32)

        per_chunk = per_batch // DC

        def q_of(b, c):
            return g.pool[:, ds(b * per_batch + start + c * per_chunk, N)]

        def k_of(b, c):
            return g.pool[:, ds(b * per_batch + start + c * per_chunk + N, N)]

        def v_chunk(b, c):
            return g.pool[:, ds(b * per_batch + start + c * per_chunk + 2 * N, VT * P)].rearrange(
                "p (t d) -> p t d", d=P)

        def v_of(b, c, t, n):
            return g.pool[:, ds(b * per_batch + start + c * per_chunk + 2 * N + t * P, n * P)].rearrange(
                "p (t d) -> p t d", d=P)

        def w1_of(e):
            return g.pool[:, ds(e * per_expert, DC * F)].rearrange("p (c f) -> p c f", c=DC)

        def w2_of(e):
            return g.pool[:, ds(e * per_expert + DC * F, FC * D)].rearrange("p (m d) -> p m d", m=FC)

        g.q_of, g.k_of, g.v_of, g.v_chunk, g.w1_of, g.w2_of = q_of, k_of, v_of, v_chunk, w1_of, w2_of
        g.tick = ctx.enter_context(nc.semaphore("tick"))
        norm_project(nc, g)
        route(nc, g)
        attend(nc, g)
        experts(nc, g)
        combine(nc, g)


def lay_out(inputs):
    import numpy as np

    arrays = {name.split("_", 2)[2]: np.ascontiguousarray(a) for name, a in inputs.items()}
    arrays["bqk_cols"] = np.ascontiguousarray(arrays["bqkv"][:2 * D].reshape(2 * DC, P).T)
    arrays["b1_cols"] = np.ascontiguousarray(arrays["b1"].reshape(E * FC, P).T)
    return arrays


def kernel(**inputs):
    import concourse.bacc as bacc
    from concourse.bass_utils import run_bass_kernel_spmd

    nc = bacc.Bacc("TRN2", target_bir_lowering=False, num_devices=1)
    arrays = lay_out(inputs)
    g = Shared({
        name: nc.dram_tensor(f"in_{name}", a.shape, mybir.dt.from_np(a.dtype), kind="ExternalInput").ap()
        for name, a in arrays.items()})
    g.out = nc.dram_tensor("out", (B, N, D), F32, kind="ExternalOutput").ap()
    build(nc, g)
    run = run_bass_kernel_spmd(nc, [{f"in_{name}": a for name, a in arrays.items()}], core_ids=[0])
    return run.results[0]["out"]
```

```python
from contextlib import ExitStack

import concourse.bass as bass
from concourse import mybir
from concourse.alu_op_type import AluOpType as ALU

F32 = mybir.dt.float32
F32R = mybir.dt.float32r
BF16 = mybir.dt.bfloat16
I32 = mybir.dt.int32
U32 = mybir.dt.uint32
ACT = mybir.ActivationFunctionType
AX = mybir.AxisListType.X

P = 128
B, N, D = 8, 512, 256
T = B * N
H, DH = 16, 16
HALF = 64
E, F = 8, 1024
DC = D // P
FC = F // P
TB = N // P
NT = T // P
VT = TB + 1
HC = P // DH
ROWS = 2 * P
STEPS = 2 * T // ROWS + E
SLOTS = STEPS * ROWS
HT = SLOTS // P
EPS = 1e-5
FAR = 3.0e38
ds = bass.ds


class Shared:

    def __init__(self, inputs):
        self.x, self.Wqkv, self.bqkv, self.bqk_cols = (inputs[n] for n in ("x", "Wqkv", "bqkv", "bqk_cols"))
        self.Wout, self.bout = inputs["Wout"], inputs["bout"]
        self.router_w, self.router_b = inputs["router_w"], inputs["router_b"]
        self.w1, self.b1_cols, self.w2, self.b2 = (inputs[n] for n in ("w1", "b1_cols", "w2", "b2"))


START = 1


def start(eng, sems):
    for sem in sems:
        eng.sem_inc(sem, START)


def wait(eng, sem, count):
    eng.wait_ge(sem, count + START)


class Chain:

    def __init__(self, eng, sem, base=0):
        self.eng, self.sem, self.count, self.base = eng, sem, 0, base

    def add(self, ins, inc=1):
        ins.then_inc(self.sem, inc)
        self.count += inc
        return self

    def value(self):
        return self.base + self.count

    def wait(self):
        wait(self.eng, self.sem, self.value())


def wait_first(eng, sem, value, tick):
    wait(eng, sem, value)
    eng.sem_inc(tick, 1)


def norm_project(nc, g):
    with ExitStack() as ctx:
        def sb(name, shape, dt=F32):
            return ctx.enter_context(nc.sbuf_tensor(name, shape, dt))

        by = {"sp": [], "pool": [], "v": [], "act": [], "pe": []}

        def sem(name, engine):
            by[engine].append(ctx.enter_context(nc.semaphore(name)))
            return by[engine][-1]

        ps = ctx.enter_context(nc.psum_tensor("ps_project", [P, 8, 512], F32))
        w_raw = sb("w_raw", [P, DC, 3 * D])
        w_hi = sb("w_hi", [P, DC, 3 * D], F32R)
        w_lo = sb("w_lo", [P, DC, 3 * D], F32R)
        rw_raw = sb("rw_raw", [P, DC, E])
        rw = sb("rw", [P, DC, 2 * E], F32R)
        rb = sb("rb", [P, E])
        b_qk = sb("b_qk", [P, 2 * DC])
        b_v = sb("b_v", [P, D])
        x = sb("x_in", [P, 2, TB, D])
        xn = sb("xn", [P, 2, TB, D])
        stats = sb("stats", [P, TB, 6])
        mv = sb("mv", [P, TB, 2])
        var = sb("var", [P, TB])
        root = sb("root", [P, TB])
        rough = sb("rough", [P, TB])
        newton = sb("newton", [P, TB])
        rstd = sb("rstd", [P, TB])
        xt_hi = sb("xt_hi", [P, 2, DC, N + 2 * HALF], F32R)
        xt_lo = sb("xt_lo", [P, 2, DC, N + 2 * HALF], F32R)
        lg = sb("lg", [P, TB, E])

        s_w = sem("s_w", "sp")
        s_whi = sem("s_whi", "act")
        s_wlo = sem("s_wlo", "v")
        s_ident = sem("s_ident", "pool")
        s_x = sem("s_x", "sp")
        s_dve = sem("s_dve", "v")
        s_var = sem("s_var", "v")
        s_root = sem("s_root", "act")
        s_tick = sem("s_tick", "v")
        s_xn = sem("s_xn", "v")
        s_xnout = sem("s_xnout", "sp")
        s_tr = sem("s_tr", "pe")
        s_hi = sem("s_hi", "act")
        s_lo = sem("s_lo", "v")
        s_lg = sem("s_lg", "pe")
        s_lgout = sem("s_lgout", "v")
        s_qk = sem("s_qk", "pe")
        s_qout = sem("s_qout", "act")
        s_kout = sem("s_kout", "v")
        s_v = sem("s_v", "pe")
        s_vout = sem("s_vout", "v")
        s_pad = sem("s_pad", "v")

        bank_t, bank_l, bank_qk, bank_v = (0, 1), 2, (3, 4), (5, 6, 7)
        v_banks = [(0, 1), (2, 3), (4,)]
        x_rows = g.x.rearrange("b (t p) d -> b p t d", p=P)
        xn_rows = g.xn_dram.rearrange("(b t p) d -> b p t d", t=TB, p=P)

        with nc.Block() as block:
            @block.sync
            def _(sp):
                start(sp, by["sp"])
                sp.dma_start(w_raw[:], g.Wqkv.rearrange("(c p) n -> p c n", p=P)).then_inc(s_w, 16)
                sp.dma_start(rw_raw[:], g.router_w.rearrange("(c p) e -> p c e", p=P)).then_inc(s_w, 16)
                sp.dma_start(rb[:], g.router_b.partition_broadcast(P)).then_inc(s_w, 16)
                sp.dma_start(b_qk[:], g.bqk_cols).then_inc(s_w, 16)
                sp.dma_start(b_v[:], g.bqkv[2 * D:3 * D].partition_broadcast(P)).then_inc(s_w, 16)

                def load(b, par):
                    sp.dma_start(x[:, par], x_rows[ds(b, 1)].rearrange("b p t d -> (b p) t d")
                                 ).then_inc(s_x, 16)

                load(0, 0)
                with sp.Fori(0, B // 2) as pair:
                    for par in range(2):
                        b = 2 * pair + par
                        following = (b + 1) % B
                        wait_first(sp, s_x, 16 * b + 16, g.tick)
                        wait_first(sp, s_xn, b, g.tick)
                        load(following, 1 - par)
                        wait_first(sp, s_xn, b + 1, g.tick)
                        wait_first(sp, s_xnout, 16 * b, g.tick)
                        sp.dma_start(xn_rows[ds(b, 1)].rearrange("b p t d -> (b p) t d"),
                                     xn[:, par]).then_inc(s_xnout, 16)
                wait(sp, s_xnout, 16 * B)
                wait(sp, s_x, 16 * (B + 1))

            @block.gpsimd
            def _(pool):
                start(pool, by["pool"])
                pool.memset(g.ident[:], 0.0).then_inc(s_ident, 1)
                wait(pool, s_ident, 1)
                pool.affine_select(out=g.ident[:], in_=g.ident[:], compare_op=ALU.not_equal, fill=1.0,
                                   base=0, pattern=[[-1, P]], channel_multiplier=1).then_inc(s_ident, 1)
            @block.vector
            def _(v):
                start(v, by["v"])
                for buf in (xt_hi, xt_lo):
                    for par in range(2):
                        for c in range(DC):
                            v.memset(buf[:, par, c, 0:HALF].bitcast(F32), 0.0).then_inc(s_pad, 1)
                            v.memset(buf[:, par, c, N + HALF:N + 2 * HALF].bitcast(F32), 0.0).then_inc(s_pad, 1)
                wait(v, s_whi, 2)
                v.tensor_tensor(w_lo[:], w_raw[:], w_hi[:].bitcast(F32), ALU.subtract).then_inc(s_wlo, 1)
                v.tensor_tensor(rw[:, :, E:2 * E], rw_raw[:], rw[:, :, 0:E].bitcast(F32),
                                ALU.subtract).then_inc(s_wlo, 1)
                with v.Fori(0, B // 2) as pair:
                    for par in range(2):
                        b = 2 * pair + par
                        chain = Chain(v, s_dve, 8 * b)
                        wait(v, s_x, 16 * (b + 1))
                        for t in range(TB):
                            ins = v.bn_stats(stats[:, t, :], x[:, par, t, :])
                        chain.add(ins)
                        wait_first(v, s_dve, chain.value(), s_tick)
                        for t in range(TB):
                            ins = v.bn_aggr(mv[:, t, :], stats[:, t, :])
                        chain.add(ins).wait()
                        v.tensor_scalar(var[:], mv[:, :, 1], EPS, None, ALU.add).then_inc(s_var, 1)
                        wait(v, s_root, b + 1)
                        chain.add(v.reciprocal(rough[:], root[:])).wait()
                        chain.add(v.tensor_tensor(newton[:], rough[:], rough[:], ALU.mult)).wait()
                        chain.add(v.tensor_tensor(newton[:], newton[:], var[:], ALU.mult)).wait()
                        chain.add(v.tensor_scalar(newton[:], newton[:], -0.5, 1.5, ALU.mult, ALU.add)).wait()
                        chain.add(v.tensor_tensor(rstd[:], rough[:], newton[:], ALU.mult)).wait()
                        wait(v, s_tr, 2 * b)
                        wait(v, s_xnout, 16 * b)
                        for t in range(TB):
                            ins = v.tensor_scalar(xn[:, par, t, :], x[:, par, t, :], mv[:, t, 0:1],
                                                  rstd[:, t:t + 1], ALU.subtract, ALU.mult)
                        ins.then_inc(s_xn, 1)
                        for c in range(DC):
                            wait(v, s_hi, 2 * b + c + 1)
                            v.tensor_tensor(xt_lo[:, par, c, HALF:HALF + N], ps[:, bank_t[c], :],
                                            xt_hi[:, par, c, HALF:HALF + N].bitcast(F32),
                                            ALU.subtract).then_inc(s_lo, 1)
                        wait(v, s_lg, b + 1)
                        lg_ps = ps[:, bank_l, 0:TB * 2 * E].rearrange("p (t e) -> p t e", t=TB)
                        chain.add(v.tensor_tensor(lg[:], lg_ps[:, :, E:2 * E],
                                                  rb[:].unsqueeze(1).to_broadcast([P, TB, E]), ALU.add)
                                  ).wait()
                        v.tensor_tensor(g.logits[:, ds(b * TB, TB), :], lg_ps[:, :, 0:E], lg[:], ALU.add
                                        ).then_inc(s_lgout, 1)
                        for m in (2, 3):
                            wait(v, s_qk, 4 * b + m + 1)
                            v.tensor_scalar(g.k_of(b, m - 2), ps[:, bank_qk[m % 2], :], b_qk[:, m:m + 1],
                                            None, ALU.add).then_inc(s_kout, 1)
                        for n, tiles in enumerate(v_banks):
                            wait(v, s_v, 3 * b + n + 1)
                            tiles_ps = ps[:, bank_v[n], 0:D * len(tiles)].rearrange("p (t d) -> p t d", d=D)
                            for c in range(DC):
                                ins = v.tensor_tensor(
                                    g.v_of(b, c, tiles[0], len(tiles)), tiles_ps[:, :, c * P:(c + 1) * P],
                                    b_v[:, c * P:(c + 1) * P].unsqueeze(1).to_broadcast([P, len(tiles), P]),
                                    ALU.add)
                            ins.then_inc(s_vout, 1)
                wait(v, s_vout, 3 * B)

            @block.scalar
            def _(act):
                start(act, by["act"])
                wait(act, s_w, 80)
                act.activation(w_hi[:], w_raw[:], ACT.Copy).then_inc(s_whi, 1)
                act.activation(rw[:, :, 0:E], rw_raw[:], ACT.Copy).then_inc(s_whi, 1)
                with act.Fori(0, B // 2) as pair:
                    for par in range(2):
                        b = 2 * pair + par
                        wait(act, s_var, b + 1)
                        act.activation(root[:], var[:], ACT.Sqrt).then_inc(s_root, 1)
                        for c in range(DC):
                            wait(act, s_tr, 2 * b + c + 1)
                            act.activation(xt_hi[:, par, c, HALF:HALF + N], ps[:, bank_t[c], :],
                                           ACT.Copy).then_inc(s_hi, 1)
                        for m in (0, 1):
                            wait(act, s_qk, 4 * b + m + 1)
                            act.activation(g.q_of(b, m), ps[:, bank_qk[m % 2], :], ACT.Identity,
                                           bias=b_qk[:, m:m + 1]).then_inc(s_qout, 1)

            @block.tensor
            def _(pe):
                start(pe, by["pe"])
                wait(pe, s_ident, 2)
                wait(pe, s_wlo, 2)
                wait(pe, s_pad, 16)
                with pe.Fori(0, B // 2) as pair:
                    for par in range(2):
                        b = 2 * pair + par
                        wait(pe, s_xn, b + 1)
                        wait(pe, s_lo, 2 * b)
                        for c in range(DC):
                            for t in range(TB):
                                ins = pe.transpose(ps[:, bank_t[c], t * P:(t + 1) * P],
                                                   xn[:, par, t, c * P:(c + 1) * P], g.ident[:])
                            ins.then_inc(s_tr, 1)
                        hi, lo = xt_hi[:, par], xt_lo[:, par]
                        wait(pe, s_lo, 2 * b + 2)
                        for m in range(4):
                            if m < 2:
                                wait(pe, s_kout, 2 * b)
                            else:
                                wait(pe, s_qout, 2 * b + m - 1)
                            n = 0
                            for c in range(DC):
                                for w, xx in ((w_hi, hi), (w_hi, lo), (w_lo, hi)):
                                    ins = pe.matmul(ps[:, bank_qk[m % 2], :], w[:, c, m * P:(m + 1) * P],
                                                    xx[:, c, HALF:HALF + N], start=(n == 0), stop=(n == 5))
                                    n += 1
                            ins.then_inc(s_qk, 1)
                        wait(pe, s_lgout, b)
                        for t in range(TB):
                            n = 0
                            for c in range(DC):
                                for xx in (hi, lo):
                                    ins = pe.matmul(ps[:, bank_l, t * 2 * E:(t + 1) * 2 * E],
                                                    xx[:, c, HALF + t * P:HALF + (t + 1) * P], rw[:, c, :],
                                                    start=(n == 0), stop=(n == 3))
                                    n += 1
                        ins.then_inc(s_lg, 1)
                        for nb, tiles in enumerate(v_banks):
                            wait(pe, s_vout, 3 * b)
                            for j, t in enumerate(tiles):
                                n = 0
                                for c in range(DC):
                                    for xx, w in ((hi, w_hi), (lo, w_hi), (hi, w_lo)):
                                        ins = pe.matmul(ps[:, bank_v[nb], j * D:(j + 1) * D],
                                                        xx[:, c, t * P:(t + 1) * P], w[:, c, 2 * D:3 * D],
                                                        start=(n == 0), stop=(n == 5))
                                        n += 1
                            ins.then_inc(s_v, 1)


def route(nc, g):
    with ExitStack() as ctx:
        def sb(name, shape, dt=F32):
            return ctx.enter_context(nc.sbuf_tensor(name, shape, dt))

        by = {"sp": [], "pool": [], "v": [], "act": [], "pe": []}

        def sem(name, engine):
            by[engine].append(ctx.enter_context(nc.semaphore(name)))
            return by[engine][-1]

        ps = ctx.enter_context(nc.psum_tensor("ps_route", [P, 4, 512], F32))
        before = sb("before", [P, P])
        ones = sb("ones", [P, P])
        expert_rank = sb("expert_rank", [P, E])
        step_iota = sb("step_iota", [P, STEPS])
        lane_iota = sb("lane_iota", [P, P], BF16)
        half_iota = sb("half_iota", [P, HT], BF16)
        lane = sb("lane", [P, 1])
        top = sb("top", [P, 2, NT])
        pick = sb("pick", [P, 2, NT, E])
        rest = sb("rest", [P, NT, E])
        tied = sb("tied", [P, NT, E])
        win = sb("win", [P, NT])
        both = sb("both", [P, NT, E])
        in_tile = sb("in_tile", [P, NT, E])
        count = sb("count", [P, E, NT])
        through = sb("through", [P, E, NT])
        place = sb("place", [P, NT, E])
        total_i = sb("total_i", [P, E], I32)
        steps_i = sb("steps_i", [P, E], I32)
        steps = sb("steps", [P, E])
        steps_end = sb("steps_end", [P, E])
        first_row = sb("first_row", [P, E])
        passed = sb("passed", [P, STEPS, E])
        expert_f = sb("expert_f", [P, STEPS])
        row = sb("row", [P, 2, NT])
        part_i = sb("part_i", [P, 2, 2, NT], I32)
        part = sb("part", [P, 2, 2, NT])
        ring = 4
        oh_lane = sb("oh_lane", [P, ring, P], BF16)
        oh_half = sb("oh_half", [P, ring, 2, HT], BF16)
        ratio = sb("ratio", [P, NT])
        denom = sb("denom", [P, NT])
        token_f = sb("token_f", [P, HT])

        s_c = sem("s_c", "pool")
        s_v = sem("s_v2", "v")
        s_pick = sem("s_pick", "v")
        s_count = sem("s_count", "pe")
        s_gap = sem("s_gap", "v")
        s_exp = sem("s_exp", "act")
        s_oh = sem("s_oh", "v")
        s_ohmm = sem("s_ohmm", "pe")

        with nc.Block() as block:
            @block.gpsimd
            def _(pool):
                start(pool, by["pool"])
                pool.memset(ones[:], 1.0).then_inc(s_c, 1)
                pool.memset(before[:], 1.0).then_inc(s_c, 1)
                pool.iota(expert_rank[:], [[-1, E]], base=E, channel_multiplier=0,
                          allow_small_or_imprecise_dtypes=True).then_inc(s_c, 1)
                pool.iota(step_iota[:], [[1, STEPS]], base=0, channel_multiplier=0,
                          allow_small_or_imprecise_dtypes=True).then_inc(s_c, 1)
                pool.iota(lane_iota[:], [[1, P]], base=0, channel_multiplier=0,
                          allow_small_or_imprecise_dtypes=True).then_inc(s_c, 1)
                pool.iota(half_iota[:], [[1, HT]], base=0, channel_multiplier=0,
                          allow_small_or_imprecise_dtypes=True).then_inc(s_c, 1)
                pool.iota(lane[:], [[0, 1]], base=0, channel_multiplier=1,
                          allow_small_or_imprecise_dtypes=True).then_inc(s_c, 1)
                wait(pool, s_c, 2)
                pool.affine_select(out=before[:], in_=before[:], compare_op=ALU.is_gt, fill=0.0, base=0,
                                   pattern=[[1, P]], channel_multiplier=-1).then_inc(s_c, 1)

            @block.vector
            def _(v):
                start(v, by["v"])
                chain = Chain(v, s_v)

                def do(ins):
                    chain.add(ins).wait()

                def per_tile(a):
                    return a.unsqueeze(2).to_broadcast([P, NT, E])

                wait(v, s_c, 8)
                rank = expert_rank[:].unsqueeze(1).to_broadcast([P, NT, E])
                for n in range(2):
                    left = g.logits[:] if n == 0 else rest[:]
                    do(v.tensor_reduce(top[:, n, :], left, AX, ALU.max))
                    do(v.tensor_tensor(tied[:], left, per_tile(top[:, n, :]), ALU.is_equal))
                    do(v.tensor_tensor(tied[:], tied[:], rank, ALU.mult))
                    do(v.tensor_reduce(win[:], tied[:], AX, ALU.max))
                    do(v.tensor_tensor(pick[:, n], rank, per_tile(win[:]), ALU.is_equal))
                    if n == 0:
                        do(v.scalar_tensor_tensor(out=rest[:], in0=pick[:, 0], scalar=-FAR, in1=left,
                                                  op0=ALU.mult, op1=ALU.add))
                v.tensor_tensor(ratio[:], top[:, 1, :], top[:, 0, :], ALU.subtract).then_inc(s_gap, 1)
                v.tensor_tensor(both[:], pick[:, 0], pick[:, 1], ALU.add).then_inc(s_pick, 1)
                wait(v, s_exp, 1)
                do(v.tensor_scalar(denom[:], ratio[:], 1.0, None, ALU.add))
                do(v.reciprocal(g.gate[:, 0, :], denom[:]))
                do(v.tensor_tensor(g.gate[:, 1, :], ratio[:], g.gate[:, 0, :], ALU.mult))
                wait(v, s_count, 2)
                v.tensor_copy(in_tile[:], ps[:, 0, 0:NT * E].rearrange("p (t e) -> p t e", e=E))
                do(v.tensor_copy(count[:], ps[:, 1, 0:NT * E].rearrange("p (t e) -> p e t", e=E)))
                for e in range(E):
                    ins = v.tensor_tensor_scan(through[:, e, :], ones[:, 0:NT], count[:, e, :], 0.0,
                                               ALU.mult, ALU.add)
                do(ins)
                do(v.tensor_scalar(total_i[:], through[:, :, NT - 1], float(ROWS - 1), None, ALU.add))
                do(v.tensor_scalar(steps_i[:], total_i[:], ROWS.bit_length() - 1, None,
                                   ALU.arith_shift_right))
                do(v.tensor_copy(steps[:], steps_i[:]))
                do(v.tensor_tensor_scan(steps_end[:], ones[:, 0:E], steps[:], 0.0, ALU.mult, ALU.add))
                do(v.tensor_tensor(first_row[:], steps_end[:], steps[:], ALU.subtract))
                do(v.tensor_scalar(first_row[:], first_row[:], float(ROWS), None, ALU.mult))
                do(v.tensor_tensor(through[:], through[:], count[:], ALU.subtract))
                do(v.tensor_tensor(place[:], in_tile[:], through[:].rearrange("p e t -> p t e"), ALU.add))
                do(v.tensor_tensor(place[:], place[:], first_row[:].unsqueeze(1).to_broadcast([P, NT, E]),
                                   ALU.add))
                do(v.tensor_tensor(passed[:], step_iota[:].unsqueeze(2).to_broadcast([P, STEPS, E]),
                                   steps_end[:].unsqueeze(1).to_broadcast([P, STEPS, E]), ALU.is_ge))
                do(v.tensor_reduce(expert_f[:], passed[:], AX, ALU.add))
                do(v.tensor_scalar(g.step_expert[:], expert_f[:], float(E - 1), None, ALU.min))
                for n in range(2):
                    do(v.tensor_tensor(rest[:], pick[:, n], place[:], ALU.mult))
                    do(v.tensor_reduce(row[:, n, :], rest[:], AX, ALU.add))
                do(v.tensor_copy(g.token_row[:], row[:]))
                v.tensor_scalar(part_i[:, 0], g.token_row[:], P.bit_length() - 1, None, ALU.arith_shift_right)
                do(v.tensor_scalar(part_i[:, 1], g.token_row[:], P - 1, None, ALU.bitwise_and))
                do(v.tensor_copy(part[:], part_i[:]))
                for n in range(2):
                    for t in range(NT):
                        at = n * NT + t
                        if at >= ring:
                            wait(v, s_ohmm, at - ring + 1)
                        half = part[:, 0, n, t:t + 1]
                        v.tensor_scalar(oh_lane[:, at % ring], lane_iota[:], part[:, 1, n, t:t + 1], None,
                                        ALU.is_equal)
                        v.tensor_scalar(oh_half[:, at % ring, 0], half_iota[:], half, float(t),
                                        ALU.is_equal, ALU.mult)
                        v.tensor_scalar(oh_half[:, at % ring, 1], half_iota[:], half, lane[:],
                                        ALU.is_equal, ALU.mult).then_inc(s_oh, 1)
                wait(v, s_ohmm, 2 * NT)
                do(v.tensor_copy(token_f[:], ps[:, 2, HT:2 * HT]))
                do(v.scalar_tensor_tensor(out=g.row_token[:], in0=ps[:, 2, 0:HT], scalar=float(P),
                                          in1=token_f[:], op0=ALU.mult, op1=ALU.add))

            @block.scalar
            def _(act):
                start(act, by["act"])
                wait(act, s_gap, 1)
                act.activation(ratio[:], ratio[:], ACT.Exp).then_inc(s_exp, 1)

            @block.tensor
            def _(pe):
                start(pe, by["pe"])
                wait(pe, s_c, 8)
                wait(pe, s_pick, 1)
                sel = both[:].rearrange("p t e -> p (t e)")
                pe.matmul(ps[:, 0, 0:NT * E], before[:], sel, start=True, stop=True).then_inc(s_count, 1)
                pe.matmul(ps[:, 1, 0:NT * E], ones[:], sel, start=True, stop=True).then_inc(s_count, 1)
                for at in range(2 * NT):
                    wait(pe, s_oh, at + 1)
                    pe.matmul(ps[:, 2, 0:2 * HT], oh_lane[:, at % ring],
                              oh_half[:, at % ring].rearrange("p a h -> p (a h)"),
                              start=(at == 0), stop=(at == 2 * NT - 1)).then_inc(s_ohmm, 1)


def attend(nc, g):
    with ExitStack() as ctx:
        def sb(name, shape, dt=F32):
            return ctx.enter_context(nc.sbuf_tensor(name, shape, dt))

        by = {"sp": [], "pool": [], "v": [], "act": [], "pe": []}

        def sem(name, engine):
            by[engine].append(ctx.enter_context(nc.semaphore(name)))
            return by[engine][-1]

        W = 2 * P
        ps = ctx.enter_context(nc.psum_tensor("ps_attend", [P, 8, 512], F32))
        wo_raw = sb("wo_raw", [P, DC, D])
        wo_hi = sb("wo_hi", [P, DC, D], F32R)
        wo_lo = sb("wo_lo", [P, DC, D], F32R)
        b_o = sb("b_o", [P, D])
        band = sb("band", [P, W])
        head_rows = sb("head_rows", [P, HC])
        q_s = sb("q_s", [P, 2, N], F32R)
        k_s = sb("k_s", [P, 2, 2, N], F32R)
        v_s = sb("v_s", [P, 2, VT, P], F32R)
        q_m = sb("q_m", [P, 2, 2, N], F32R)
        v_m = sb("v_m", [P, 2, 2, VT, P], F32R)
        wt = g.pool[:, 0:2 * TB * W].rearrange("p (r t w) -> p r t w", r=2, t=TB)
        low = sb("low", [P, 2, TB])
        total = sb("total", [P, DC, TB, HC])
        inv_s = sb("inv_s", [P, TB, HC])
        inv = sb("inv", [P, TB, HC, DH])
        inv_t = sb("inv_t", [P, N])
        pt = sb("pt", [P, 2, 2, 2, N], F32R)
        a_hi = sb("a_hi", [P, DC, N], F32R)
        a_lo = sb("a_lo", [P, DC, N], F32R)
        xb = sb("xb", [P, TB, D])

        s_in = sem("s_in", "sp")
        s_const = sem("s_const", "pool")
        s_wohi = sem("s_wohi", "act")
        s_wolo = sem("s_wolo", "v")
        s_xb = sem("s_xb", "sp")
        s_out = sem("s_out", "sp")
        s_wload = sem("s_wload", "sp")
        s_hi = sem("s_hi3", "act")
        s_lo = sem("s_lo3", "v")
        s_vhi = sem("s_vhi", "act")
        s_vlo = sem("s_vlo", "v")
        s_qm = sem("s_qm", "v")
        s_vz = sem("s_vz", "pool")
        s_vm = sem("s_vm", "pool")
        s_s = sem("s_s", "pe")
        s_low = sem("s_low", "v")
        s_exp = sem("s_exp3", "act")
        s_t = sem("s_t", "pe")
        s_phi = sem("s_phi", "act")
        s_plo = sem("s_plo", "v")
        s_pv = sem("s_pv", "pe")
        s_rec = sem("s_rec", "v")
        s_inv = sem("s_inv", "v")
        s_invt = sem("s_invt", "pe")
        s_invs = sem("s_invs", "act")
        s_a = sem("s_a", "v")
        s_ahi = sem("s_ahi", "act")
        s_alo = sem("s_alo", "v")
        s_proj = sem("s_proj", "pe")
        s_done = sem("s_done", "v")
        s_biased = sem("s_biased", "v")

        bank_s, bank_t, bank_o, bank_m = ((0, 1), (2, 3)), (4, 5), 6, 7
        heads = DC * HC
        x_rows = g.x.rearrange("b (t p) d -> b p t d", p=P)
        base_rows = g.base_dram.rearrange("(b t p) d -> b p t d", t=TB, p=P)

        def window(i):
            begin = max(0, HALF - P * i)
            end = min(W, N + HALF - P * i)
            return begin, end, begin + P * i - HALF

        def chunk_of(b, k):
            c = k // HC
            return (b, c) if c < DC else ((b + 1) % B | b // (B - 1) * (B - 1), c - DC)

        def each_batch(eng, batch):
            batch(0, True)
            with eng.Fori(1, B) as b:
                batch(b, False)

        with nc.Block() as block:
            @block.sync
            def _(sp):
                start(sp, by["sp"])
                sp.dma_start(wo_raw[:], g.Wout.rearrange("(c p) n -> p c n", p=P)).then_inc(s_in, 16)
                sp.dma_start(b_o[:], g.bout.partition_broadcast(P)).then_inc(s_in, 16)

                def load_w1(e):
                    sp.dma_start(g.w1_of(e), g.w1[ds(e, 1)].rearrange("e (c p) f -> (e p) c f", p=P)
                                 ).then_inc(s_wload, 16)

                def batch(b, first):
                    if not first:
                        wait_first(sp, s_out, 16 * b, g.tick)
                    sp.dma_start(xb[:], x_rows[ds(b, 1)].rearrange("b p t d -> (b p) t d")).then_inc(s_xb, 16)
                    wait_first(sp, s_done, 2 * b + 2, g.tick)
                    sp.dma_start(base_rows[ds(b, 1)].rearrange("b p t d -> (b p) t d"), xb[:]).then_inc(s_out, 16)
                    if not first:
                        wait_first(sp, s_wload, 32 * b - 16, g.tick)
                        load_w1(b)
                    sp.dma_start(g.w2_of(b), g.w2[ds(b, 1)].rearrange("e (m p) d -> (e p) m d", p=P)
                                 ).then_inc(s_wload, 16)

                each_batch(sp, batch)
                load_w1(0)
                wait(sp, s_out, 16 * B)
                wait(sp, s_wload, 32 * E)

            @block.gpsimd
            def _(pool):
                start(pool, by["pool"])
                pool.memset(band[:], 0.0).then_inc(s_vz, 1)
                pool.memset(head_rows[:], 1.0).then_inc(s_vz, 1)
                wait(pool, s_vz, 2)
                pool.affine_select(out=band[:], in_=band[:], compare_op=ALU.is_ge, fill=FAR, base=0,
                                   pattern=[[1, W]], channel_multiplier=-1).then_inc(s_vz, 1)
                pool.affine_select(out=head_rows[:], in_=head_rows[:], compare_op=ALU.is_ge, fill=0.0,
                                   base=0, pattern=[[-DH, HC]], channel_multiplier=1).then_inc(s_vz, 1)
                wait(pool, s_vz, 4)
                pool.affine_select(out=band[:], in_=band[:], compare_op=ALU.is_ge, fill=FAR, base=2 * HALF,
                                   pattern=[[-1, W]], channel_multiplier=1).then_inc(s_const, 1)
                pool.affine_select(out=head_rows[:], in_=head_rows[:], compare_op=ALU.is_ge, fill=0.0,
                                   base=DH - 1, pattern=[[DH, HC]], channel_multiplier=-1).then_inc(s_const, 1)
                for ring in range(2):
                    pool.memset(v_m[:, ring].bitcast(F32), 0.0).then_inc(s_const, 1)
                pool.memset(wt[:, :, 0, 0:HALF], 0.0).then_inc(s_const, 1)
                pool.memset(wt[:, :, TB - 1, W - HALF:W], 0.0).then_inc(s_const, 1)
                wait(pool, s_const, 6)

                def batch(b, first):
                    for n in range(heads):
                        m, j, ring = heads * b + n, n % HC, n % 2
                        if j == 0:
                            wait_first(pool, s_vlo, 2 * b + n // HC + 1, g.tick)
                        if not (first and n < 2):
                            wait_first(pool, s_pv, m - 1, g.tick)
                        old = DH * ((j - 2) % HC)
                        pool.memset(v_m[:, ring, :, :, old:old + DH].rearrange("p h t d -> p (h t) d").bitcast(F32), 0.0)
                        pool.tensor_copy(v_m[:, ring, :, :, DH * j:DH * (j + 1)].rearrange("p h t d -> p (h t) d"),
                                         v_s[:, :, :, DH * j:DH * (j + 1)].rearrange("p h t d -> p (h t) d")
                                         ).then_inc(s_vm, 1)

                each_batch(pool, batch)

            @block.vector
            def _(v):
                start(v, by["v"])

                def lo_of_chunk(b, k):
                    u, (src, c) = 2 * b + k // HC, chunk_of(b, k)
                    wait(v, s_hi, u + 1)
                    v.scalar_tensor_tensor(out=q_s[:, 1], in0=g.q_of(src, c), scalar=-DH ** -0.5,
                                           in1=q_s[:, 0].bitcast(F32), op0=ALU.mult, op1=ALU.subtract)
                    v.tensor_tensor(k_s[:, c, 1], g.k_of(src, c), k_s[:, c, 0].bitcast(F32), ALU.subtract
                                    ).then_inc(s_lo, 1)

                def lo_of_values(b, k):
                    u, (src, c) = 2 * b + k // HC, chunk_of(b, k)
                    wait(v, s_vhi, u + 1)
                    v.tensor_tensor(v_s[:, 1], g.v_chunk(src, c), v_s[:, 0].bitcast(F32), ALU.subtract
                                    ).then_inc(s_vlo, 1)

                def one_head(b, k, fresh=False):
                    m, j, ring = heads * b + k, k % HC, k % 2
                    if not fresh:
                        wait(v, s_s, m - 1)
                    if j == 0:
                        wait(v, s_lo, 2 * b + k // HC + 1)
                    v.tensor_scalar(q_m[:, ring], q_s[:].bitcast(F32), head_rows[:, j:j + 1], None,
                                    ALU.mult).then_inc(s_qm, 1)

                def mask(b, k, fresh=False):
                    m, ring = heads * b + k, k % 2
                    wait(v, s_s, m + 1)
                    if not fresh:
                        wait_first(v, s_t, 2 * m - 2, g.tick)
                    for i in range(TB):
                        f, l, _ = window(i)
                        bank = bank_s[ring][i // 2]
                        ins = v.tensor_tensor_reduce(
                            out=wt[:, ring, i, f:l], in0=ps[:, bank, W * (i % 2) + f:W * (i % 2) + l],
                            in1=band[:, f:l], scale=1.0, scalar=FAR, op0=ALU.add, op1=ALU.min,
                            accum_out=low[:, ring, i:i + 1])
                    ins.then_inc(s_low, 1)

                def lo_of_weights(b, k):
                    m, (hi, lo) = heads * b + k, (pt[:, k % 2, 0], pt[:, k % 2, 1])
                    for h in range(2):
                        wait(v, s_phi, 2 * m + h + 1)
                        v.tensor_tensor(lo[:, h], ps[:, bank_t[h], :], hi[:, h].bitcast(F32),
                                        ALU.subtract).then_inc(s_plo, 1)

                def invert(b, c):
                    u = 2 * b + c
                    wait(v, s_exp, heads * b + HC * (c + 1))
                    v.reciprocal(inv_s[:], total[:, c]).then_inc(s_rec, 1)
                    wait(v, s_rec, u + 1)
                    v.tensor_copy(inv[:], inv_s[:].unsqueeze(3).to_broadcast([P, TB, HC, DH])).then_inc(s_inv, 1)

                def normalise(u):
                    wait(v, s_pv, HC * (u + 1))
                    wait(v, s_invs, u + 1)
                    v.tensor_tensor(inv_t[:], ps[:, bank_o, :], inv_t[:], ALU.mult).then_inc(s_a, 1)

                def lo_of_output(u, c):
                    wait(v, s_ahi, u + 1)
                    v.tensor_tensor(a_lo[:, c], inv_t[:], a_hi[:, c].bitcast(F32), ALU.subtract).then_inc(s_alo, 1)

                def add_projected(b, h):
                    wait(v, s_biased, b + 1)
                    wait(v, s_proj, 2 * b + h + 1)
                    v.tensor_tensor(xb[:, 2 * h:2 * h + 2], ps[:, bank_m, :].rearrange("p (t d) -> p t d", d=D),
                                    xb[:, 2 * h:2 * h + 2], ALU.add).then_inc(s_done, 1)

                wait(v, s_wohi, 1)
                v.tensor_tensor(wo_lo[:], wo_raw[:], wo_hi[:].bitcast(F32), ALU.subtract).then_inc(s_wolo, 1)
                wait(v, s_const, 6)
                lo_of_chunk(0, 0)
                one_head(0, 0, True)
                one_head(0, 1, True)
                mask(0, 0, True)
                one_head(0, 2)
                mask(0, 1, True)

                def batch(b, first):
                    for n in range(heads):
                        if n % HC == 0:
                            lo_of_values(b, n)
                        lo_of_weights(b, n)
                        mask(b, n + 2)
                        if n % HC == 0 and not (first and n == 0):
                            normalise(2 * b + n // HC - 1)
                        if n % HC == 1 and not (first and n == 1):
                            lo_of_output(2 * b + n // HC - 1, (n // HC - 1) % DC)
                        if n in (3, 5) and not first:
                            add_projected(b - 1, (n - 3) // 2)
                        if n % HC == HC - 3:
                            lo_of_chunk(b, n + 3)
                        if n == 12:
                            wait(v, s_xb, 16 * b + 16)
                            v.tensor_tensor(xb[:], xb[:], b_o[:].unsqueeze(1).to_broadcast([P, TB, D]),
                                            ALU.add).then_inc(s_biased, 1)
                        one_head(b, n + 3)
                        if n % HC == HC - 1:
                            invert(b, n // HC)

                each_batch(v, batch)
                normalise(2 * B - 1)
                lo_of_output(2 * B - 1, DC - 1)
                add_projected(B - 1, 0)
                add_projected(B - 1, 1)

            @block.scalar
            def _(act):
                start(act, by["act"])

                def hi_of_chunk(b, k):
                    src, c = chunk_of(b, k)
                    if k:
                        wait_first(act, s_qm, heads * b + k, g.tick)
                        wait_first(act, s_s, heads * b + k - HC, g.tick)
                    act.activation(q_s[:, 0], g.q_of(src, c), ACT.Copy, scale=-DH ** -0.5)
                    act.activation(k_s[:, c, 0], g.k_of(src, c), ACT.Copy).then_inc(s_hi, 1)

                def hi_of_values(b, k):
                    src, c = chunk_of(b, k)
                    if k:
                        wait_first(act, s_vm, heads * b + k, g.tick)
                    act.activation(v_s[:, 0], g.v_chunk(src, c), ACT.Copy).then_inc(s_vhi, 1)

                def exponentials(b, k):
                    m, c, j, ring = heads * b + k, k // HC % DC, k % HC, k % 2
                    if j == 0 and k:
                        wait(act, s_inv, 2 * b + k // HC - 1)
                    wait(act, s_low, m + 1)
                    for i in range(TB):
                        f, l, _ = window(i)
                        ins = act.activation(wt[:, ring, i, f:l], wt[:, ring, i, f:l], ACT.Exp,
                                             bias=low[:, ring, i:i + 1], scale=-1.0,
                                             accum_out=total[:, c, i, j:j + 1])
                    ins.then_inc(s_exp, 1)

                def hi_of_weights(b, k, fresh):
                    m = heads * b + k
                    if not fresh:
                        wait(act, s_pv, m - 1)
                    for h in range(2):
                        wait(act, s_t, 2 * m + h + 1)
                        act.activation(pt[:, k % 2, 0, h], ps[:, bank_t[h], :], ACT.Copy).then_inc(s_phi, 1)

                def inverse_out(u, fresh):
                    wait(act, s_invt, u + 1)
                    if not fresh:
                        wait(act, s_alo, u)
                    act.activation(inv_t[:], ps[:, bank_m, :], ACT.Copy).then_inc(s_invs, 1)

                def hi_of_output(u, c, fresh):
                    wait(act, s_a, u + 1)
                    if not fresh:
                        wait(act, s_proj, u - c)
                    act.activation(a_hi[:, c], inv_t[:], ACT.Copy).then_inc(s_ahi, 1)

                wait(act, s_in, 32)
                act.activation(wo_hi[:], wo_raw[:], ACT.Copy).then_inc(s_wohi, 1)
                wait(act, s_const, 6)
                hi_of_chunk(0, 0)
                hi_of_values(0, 0)
                exponentials(0, 0)
                exponentials(0, 1)

                def batch(b, first):
                    for n in range(heads):
                        hi_of_weights(b, n, first and n < 2)
                        if n % HC == 0 and not (first and n == 0):
                            inverse_out(2 * b + n // HC - 1, first and n == HC)
                        if n % HC == 1 and not (first and n == 1):
                            hi_of_output(2 * b + n // HC - 1, (n // HC - 1) % DC, first)
                        if n % HC == HC - 3:
                            hi_of_chunk(b, n + 3)
                        exponentials(b, n + 2)
                        if n % HC == HC - 1:
                            hi_of_values(b, n + 1)

                each_batch(act, batch)
                inverse_out(2 * B - 1, False)
                hi_of_output(2 * B - 1, DC - 1, False)

            @block.tensor
            def _(pe):
                start(pe, by["pe"])

                def scores(b, k, fresh=False):
                    m, c, ring = heads * b + k, k // HC % DC, k % 2
                    wait(pe, s_qm, m + 1)
                    if not fresh:
                        wait(pe, s_low, m - 1)
                    if k % HC == 0:
                        wait(pe, s_lo, 2 * b + k // HC + 1)
                    for i in range(TB):
                        f, l, key = window(i)
                        for p, (a, kk) in enumerate(((0, 0), (0, 1), (1, 0))):
                            ins = pe.matmul(ps[:, bank_s[ring][i // 2], W * (i % 2) + f:W * (i % 2) + l],
                                            q_m[:, ring, a, i * P:(i + 1) * P],
                                            k_s[:, c, kk, key:key + l - f], start=(p == 0), stop=(p == 2))
                    ins.then_inc(s_s, 1)

                def transposes(b, k, fresh):
                    m, ring = heads * b + k, k % 2
                    wait(pe, s_exp, m + 1)
                    for i in range(TB):
                        if i % 2 == 0 and not fresh:
                            wait(pe, s_plo, 2 * m + i // 2 - 1)
                        for h in range(2):
                            at = (2 * i + h) % TB
                            ins = pe.transpose(ps[:, bank_t[i // 2], at * P:(at + 1) * P],
                                               wt[:, ring, i, h * P:(h + 1) * P], g.ident[:])
                        if i % 2:
                            ins.then_inc(s_t, 1)

                def weighted_values(b, k):
                    m, j, ring = heads * b + k, k % HC, k % 2
                    wait(pe, s_vm, m + 1)
                    wait(pe, s_plo, 2 * m + 2)
                    if j == 0:
                        wait(pe, s_a, 2 * b + k // HC)
                    hi = pt[:, ring, 0].rearrange("p h n -> p (h n)")
                    lo = pt[:, ring, 1].rearrange("p h n -> p (h n)")
                    for t in range(VT):
                        a, z = max(0, (2 * t - 1) * P), min(2 * N, (2 * t + 1) * P)
                        o = max(0, (t - 1) * P)
                        for p, (vv, w) in enumerate(((0, hi), (0, lo), (1, hi))):
                            ins = pe.matmul(ps[:, bank_o, o:o + z - a], v_m[:, ring, vv, t, :], w[:, a:z],
                                            start=(j == 0 and t == 0 and p == 0),
                                            stop=(j == HC - 1 and t == VT - 1 and p == 2),
                                            skip_group_check=True)
                    ins.then_inc(s_pv, 1)

                def transpose_inverse(u):
                    wait(pe, s_inv, u + 1)
                    for i in range(TB):
                        ins = pe.transpose(ps[:, bank_m, i * P:(i + 1) * P],
                                           inv[:, i].rearrange("p h d -> p (h d)"), g.ident[:])
                    ins.then_inc(s_invt, 1)

                def project(b, h):
                    wait(pe, s_alo, 2 * b + 2)
                    wait(pe, s_done, 2 * b + h)
                    for t in range(2):
                        k = 0
                        tok = (2 * h + t) * P
                        for c in range(DC):
                            for a, w in ((a_hi, wo_hi), (a_lo, wo_hi), (a_hi, wo_lo)):
                                ins = pe.matmul(ps[:, bank_m, t * D:(t + 1) * D], a[:, c, tok:tok + P],
                                                w[:, c, :], start=(k == 0), stop=(k == 5))
                                k += 1
                    ins.then_inc(s_proj, 1)

                wait(pe, s_wolo, 1)
                wait(pe, s_const, 6)
                scores(0, 0, True)
                scores(0, 1, True)

                def batch(b, first):
                    for n in range(heads):
                        after_first = not (first and n == 0)
                        transposes(b, n, not after_first)
                        if n % HC == 0 and after_first:
                            transpose_inverse(2 * b + n // HC - 1)
                        scores(b, n + 2)
                        if after_first:
                            weighted_values(b, n - 1)
                        if n in (2, 4) and not first:
                            project(b - 1, (n - 2) // 2)

                each_batch(pe, batch)
                transpose_inverse(2 * B - 1)
                weighted_values(B - 1, heads - 1)
                project(B - 1, 0)
                project(B - 1, 1)


def experts(nc, g):
    with ExitStack() as ctx:
        def sb(name, shape, dt=F32):
            return ctx.enter_context(nc.sbuf_tensor(name, shape, dt))

        by = {"sp": [], "pool": [], "v": [], "act": [], "pe": []}

        def sem(name, engine):
            by[engine].append(ctx.enter_context(nc.semaphore(name)))
            return by[engine][-1]

        def dma_sem(name):
            return ctx.enter_context(nc.semaphore(name))

        ps = ctx.enter_context(nc.psum_tensor("ps_experts", [P, 8, 512], F32))
        w1_hi = sb("w1_hi", [P, DC, F], F32R)
        w1_lo = sb("w1_lo", [P, DC, F], F32R)
        w2_hi = sb("w2_hi", [P, FC, D], F32R)
        w2_lo = sb("w2_lo", [P, FC, D], F32R)
        b1 = sb("b1_s", [P, E * FC])
        b2 = sb("b2_s", [P, E, D])
        index = sb("index", [P, 2, 2], U32)
        xg = sb("xg", [P, 2, 2, D])
        xt_hi = sb("xgt_hi", [P, DC, ROWS], F32R)
        xt_lo = sb("xgt_lo", [P, DC, ROWS], F32R)
        hid = sb("hid", [P, 2, 2, ROWS])
        h_hi = sb("h_hi", [P, FC, ROWS], F32R)
        h_lo = sb("h_lo", [P, FC, ROWS], F32R)
        y = sb("y", [P, 2, 2, D])

        s_in = sem("s_in4", "sp")
        s_idx = sem("s_idx", "pool")
        s_g = [dma_sem("s_g0"), dma_sem("s_g1")]
        s_tr = sem("s_tr4", "pe")
        s_xhi = sem("s_xhi", "act")
        s_xlo = sem("s_xlo", "v")
        s_w1hi = sem("s_w1hi", "act")
        s_w1lo = sem("s_w1lo", "v")
        s_w2hi = sem("s_w2hi", "act")
        s_w2lo = sem("s_w2lo", "v")
        s_l1 = sem("s_l1", "pe")
        s_hid = sem("s_hid", "act")
        s_hhi = sem("s_hhi", "v")
        s_h = sem("s_h", "v")
        s_l2 = sem("s_l2", "pe")
        s_y = sem("s_y", "v")
        s_yout = sem("s_yout", "sp")

        bank_h, bank_t, bank_y = (0, 1, 2, 3), 4, (5, 6)
        FG, MG = F // 2, FC // 2
        y_rows = g.y_dram.rearrange("(s h p) d -> s p h d", h=2, p=P)

        def expert_of(eng, s):
            return eng.value_load(g.step_expert[0:1, ds(s, 1)], min_val=0, max_val=E - 1)

        with nc.Block() as block:
            @block.sync
            def _(sp):
                start(sp, by["sp"])
                sp.dma_start(b1[:], g.b1_cols).then_inc(s_in, 16)
                sp.dma_start(b2[:], g.b2.partition_broadcast(P)).then_inc(s_in, 16)
                with sp.Fori(0, STEPS // 2) as pair:
                    for par in range(2):
                        s = 2 * pair + par
                        wait_first(sp, s_yout, 16 * s, g.tick)
                        wait_first(sp, s_y, s + 1, g.tick)
                        sp.dma_start(y_rows[ds(s, 1)].rearrange("s p h d -> (s p) h d"), y[:, par]
                                     ).then_inc(s_yout, 16)
                wait(sp, s_yout, 16 * STEPS)

            @block.gpsimd
            def _(pool):
                start(pool, by["pool"])
                def gather(s, row_step, ring):
                    pool.tensor_copy(index[:, ring], g.row_token[:, ds(2 * row_step, 2)]).then_inc(s_idx, 1)
                    wait_first(pool, s_idx, s + 1, g.tick)
                    for h in range(2):
                        pool.indirect_dma_start(
                            xg[:, ring, h], None, g.xn_dram,
                            bass.IndirectOffsetOnAxis(ap=index[:, ring, h:h + 1], axis=0)
                            ).then_inc(s_g[h], 16)

                gather(0, 0, 0)
                with pool.Fori(0, STEPS // 2) as pair:
                    for par in range(2):
                        s = 2 * pair + par
                        for h in range(2):
                            pool.wait_ge(s_g[h], 16 * s + 16)
                            pool.sem_inc(g.tick, 1)
                        wait_first(pool, s_tr, s, g.tick)
                        gather(s + 1, (s + 1) % STEPS, 1 - par)
                for h in range(2):
                    pool.wait_ge(s_g[h], 16 * (STEPS + 1))

            @block.vector
            def _(v):
                start(v, by["v"])
                def lo_of_w1(s, e, n):
                    wait(v, s_w1hi, 2 * s + n + 1)
                    cols = slice(n * FG, (n + 1) * FG)
                    v.tensor_tensor(w1_lo[:, :, cols], g.w1_of(e)[:, :, cols], w1_hi[:, :, cols].bitcast(F32),
                                    ALU.subtract).then_inc(s_w1lo, 1)

                def lo_of_w2(s, e, n):
                    wait(v, s_w2hi, 2 * s + n + 1)
                    m = slice(n * MG, (n + 1) * MG)
                    v.tensor_tensor(w2_lo[:, m], g.w2_of(e)[:, m], w2_hi[:, m].bitcast(F32),
                                    ALU.subtract).then_inc(s_w2lo, 1)

                def lo_of_rows(s):
                    wait(v, s_xhi, s + 1)
                    v.tensor_tensor(xt_lo[:].rearrange("p c n -> p (c n)"), ps[:, bank_t, :],
                                    xt_hi[:].rearrange("p c n -> p (c n)").bitcast(F32),
                                    ALU.subtract).then_inc(s_xlo, 1)

                def hidden(s, n):
                    wait(v, s_hid, 4 * s + n + 1)
                    v.tensor_copy(h_hi[:, 2 * n:2 * n + 2], hid[:, n % 2]).then_inc(s_hhi, 1)
                    wait(v, s_hhi, 4 * s + n + 1)
                    v.tensor_tensor(h_lo[:, 2 * n:2 * n + 2], hid[:, n % 2],
                                    h_hi[:, 2 * n:2 * n + 2].bitcast(F32), ALU.subtract).then_inc(s_h, 1)

                wait(v, s_in, 32)
                first = expert_of(v, 0)
                lo_of_w1(0, first, 0)
                lo_of_rows(0)
                lo_of_w1(0, first, 1)
                lo_of_w2(0, first, 0)
                with v.Fori(0, STEPS // 2) as pair:
                    for par in range(2):
                        s = 2 * pair + par
                        e, e_next = expert_of(v, s), expert_of(v, (s + 1) % STEPS)
                        hidden(s, 0)
                        hidden(s, 1)
                        lo_of_w2(s, e, 1)
                        hidden(s, 2)
                        hidden(s, 3)
                        lo_of_w1(s + 1, e_next, 0)
                        lo_of_rows(s + 1)
                        lo_of_w1(s + 1, e_next, 1)
                        lo_of_w2(s + 1, e_next, 0)
                        wait(v, s_l2, 2 * s + 2)
                        wait(v, s_yout, 16 * s)
                        v.tensor_tensor(y[:, par], ps[:, bank_y[0]:bank_y[1] + 1, 0:D],
                                        b2[:, ds(e, 1), :].to_broadcast([P, 2, D]), ALU.add).then_inc(s_y, 1)

            @block.scalar
            def _(act):
                start(act, by["act"])
                def hi_of_w1(e, n):
                    cols = slice(n * FG, (n + 1) * FG)
                    act.activation(w1_hi[:, :, cols], g.w1_of(e)[:, :, cols], ACT.Copy).then_inc(s_w1hi, 1)

                def hi_of_w2(e, n):
                    m = slice(n * MG, (n + 1) * MG)
                    act.activation(w2_hi[:, m], g.w2_of(e)[:, m], ACT.Copy).then_inc(s_w2hi, 1)

                def hi_of_rows(s):
                    wait_first(act, s_tr, s + 1, g.tick)
                    act.activation(xt_hi[:].rearrange("p c n -> p (c n)"), ps[:, bank_t, :], ACT.Copy
                                   ).then_inc(s_xhi, 1)

                def hidden(s, e, n):
                    wait_first(act, s_l1, 4 * s + n + 1, g.tick)
                    wait_first(act, s_h, 4 * s + n - 1 if n > 1 else 4 * s, g.tick)
                    for j in range(2):
                        ins = act.activation(hid[:, n % 2, j], ps[:, bank_h[n], j * ROWS:(j + 1) * ROWS],
                                             ACT.Relu, bias=b1[:, ds(e * FC + 2 * n + j, 1)])
                    ins.then_inc(s_hid, 1)

                wait(act, s_in, 32)
                first = expert_of(act, 0)
                hi_of_w1(first, 0)
                hi_of_rows(0)
                hi_of_w1(first, 1)
                hi_of_w2(first, 0)
                with act.Fori(0, STEPS // 2) as pair:
                    for par in range(2):
                        s = 2 * pair + par
                        e, e_next = expert_of(act, s), expert_of(act, (s + 1) % STEPS)
                        hidden(s, e, 0)
                        hi_of_w2(e, 1)
                        hidden(s, e, 1)
                        hidden(s, e, 2)
                        hidden(s, e, 3)
                        hi_of_w1(e_next, 0)
                        hi_of_rows(s + 1)
                        hi_of_w1(e_next, 1)
                        wait_first(act, s_l2, 2 * s + 1, g.tick)
                        hi_of_w2(e_next, 0)

            @block.tensor
            def _(pe):
                start(pe, by["pe"])
                def transpose_rows(s, ring):
                    for h in range(2):
                        pe.wait_ge(s_g[h], 16 * s + 16)
                    wait(pe, s_xlo, s)
                    for c in range(DC):
                        for h in range(2):
                            ins = pe.transpose(ps[:, bank_t, (c * 2 + h) * P:(c * 2 + h + 1) * P],
                                               xg[:, ring, h, c * P:(c + 1) * P], g.ident[:])
                    ins.then_inc(s_tr, 1)

                transpose_rows(0, 0)
                with pe.Fori(0, STEPS // 2) as pair:
                    for par in range(2):
                        s = 2 * pair + par
                        wait(pe, s_xlo, s + 1)
                        wait(pe, s_hid, 4 * s)
                        for m in range(FC):
                            if m % MG == 0:
                                wait(pe, s_w1lo, 2 * s + m // MG + 1)
                            k = 0
                            for c in range(DC):
                                for w, xx in ((w1_hi, xt_hi), (w1_hi, xt_lo), (w1_lo, xt_hi)):
                                    ins = pe.matmul(ps[:, bank_h[m // 2], m % 2 * ROWS:(m % 2 + 1) * ROWS],
                                                    w[:, c, m * P:(m + 1) * P], xx[:, c, :],
                                                    start=(k == 0), stop=(k == 5))
                                    k += 1
                            if m % 2:
                                ins.then_inc(s_l1, 1)
                        wait(pe, s_y, s)
                        transpose_rows(s + 1, 1 - par)
                        for m in range(FC):
                            if m % MG == 0:
                                wait(pe, s_w2lo, 2 * s + m // MG + 1)
                            if m % 2 == 0:
                                wait(pe, s_h, 4 * s + m // 2 + 1)
                            for h in range(2):
                                for k, (a, w) in enumerate(((h_hi, w2_hi), (h_lo, w2_hi), (h_hi, w2_lo))):
                                    ins = pe.matmul(ps[:, bank_y[h], 0:D], a[:, m, h * P:(h + 1) * P], w[:, m, :],
                                                    start=(m == 0 and k == 0), stop=(m == FC - 1 and k == 2))
                            if m % MG == MG - 1:
                                ins.then_inc(s_l2, 1)


def combine(nc, g):
    with ExitStack() as ctx:
        def sb(name, shape, dt=F32):
            return ctx.enter_context(nc.sbuf_tensor(name, shape, dt))

        by = {"sp": [], "pool": [], "v": [], "act": [], "pe": []}

        def sem(name, engine):
            by[engine].append(ctx.enter_context(nc.semaphore(name)))
            return by[engine][-1]

        def dma_sem(name):
            return ctx.enter_context(nc.semaphore(name))

        index = sb("index5", [P, 2, 2, TB], U32)
        base = sb("base", [P, 2, TB, D])
        rows = sb("rows", [P, 2, 2, TB, D])
        s_idx = sem("s_idx5", "pool")
        s_base = sem("s_base", "sp")
        s_g = [[dma_sem(f"s_rows{n}{t}") for t in range(TB)] for n in range(2)]
        s_sum = sem("s_sum", "v")
        s_sent = sem("s_sent", "sp")

        base_rows = g.base_dram.rearrange("(b t p) d -> b p t d", t=TB, p=P)
        out_rows = g.out.rearrange("b (t p) d -> b p t d", p=P)

        with nc.Block() as block:
            @block.sync
            def _(sp):
                start(sp, by["sp"])
                def load(b, par):
                    sp.dma_start(base[:, par], base_rows[ds(b, 1)].rearrange("b p t d -> (b p) t d")
                                 ).then_inc(s_base, 16)

                load(0, 0)
                with sp.Fori(0, B // 2) as pair:
                    for par in range(2):
                        b = 2 * pair + par
                        following = (b + 1) % B
                        wait_first(sp, s_base, 16 * b + 16, g.tick)
                        wait_first(sp, s_sent, 16 * b, g.tick)
                        load(following, 1 - par)
                        wait_first(sp, s_sum, 4 * b + 4, g.tick)
                        sp.dma_start(out_rows[ds(b, 1)].rearrange("b p t d -> (b p) t d"), base[:, par]
                                     ).then_inc(s_sent, 16)
                wait(sp, s_sent, 16 * B)
                wait(sp, s_base, 16 * (B + 1))

            @block.gpsimd
            def _(pool):
                start(pool, by["pool"])
                def gather(count, b, ring):
                    pool.tensor_copy(index[:, ring], g.token_row[:, :, ds(b * TB, TB)]).then_inc(s_idx, 1)
                    wait_first(pool, s_idx, count, g.tick)
                    for t in range(TB):
                        for n in range(2):
                            pool.indirect_dma_start(
                                rows[:, ring, n, t], None, g.y_dram,
                                bass.IndirectOffsetOnAxis(ap=index[:, ring, n, t:t + 1], axis=0)
                                ).then_inc(s_g[n][t], 16)

                gather(1, 0, 0)
                with pool.Fori(0, B // 2) as pair:
                    for par in range(2):
                        b = 2 * pair + par
                        for n in range(2):
                            for t in range(TB):
                                pool.wait_ge(s_g[n][t], 16 * b + 16)
                                pool.sem_inc(g.tick, 1)
                        wait_first(pool, s_sum, 4 * b, g.tick)
                        gather(b + 2, (b + 1) % B, 1 - par)
                for n in range(2):
                    for t in range(TB):
                        pool.wait_ge(s_g[n][t], 16 * (B + 1))

            @block.vector
            def _(v):
                start(v, by["v"])
                with v.Fori(0, B // 2) as pair:
                    for par in range(2):
                        b = 2 * pair + par
                        chain = Chain(v, s_sum, 4 * b)
                        for n in range(2):
                            for t in range(TB):
                                v.wait_ge(s_g[n][t], 16 * b + 16)
                            gate = g.gate[:, n, ds(b * TB, TB)].unsqueeze(2).to_broadcast([P, TB, D])
                            chain.add(v.tensor_tensor(rows[:, par, n], rows[:, par, n], gate, ALU.mult))
                        wait(v, s_base, 16 * b + 16)
                        chain.wait()
                        chain.add(v.tensor_tensor(rows[:, par, 0], rows[:, par, 0], rows[:, par, 1], ALU.add)).wait()
                        chain.add(v.tensor_tensor(base[:, par], base[:, par], rows[:, par, 0], ALU.add))


def build(nc, g):
    with ExitStack() as ctx:
        def sb(name, shape, dt=F32):
            return ctx.enter_context(nc.sbuf_tensor(name, shape, dt))

        g.base_dram = nc.dram_tensor("base_rows", (T, D), F32).ap()
        g.xn_dram = nc.dram_tensor("xn_rows", (T, D), F32).ap()
        g.y_dram = nc.dram_tensor("expert_rows", (SLOTS, D), F32).ap()
        per_expert = DC * F + FC * D
        per_batch = 2 * DC * N + VT * D
        g.pool = sb("weights_qkv", [P, E * per_expert])
        start = E * per_expert - B * per_batch
        g.ident = sb("ident", [P, P])
        g.logits = sb("logits", [P, NT, E])
        g.gate = sb("gate", [P, 2, NT])
        g.token_row = sb("token_row", [P, 2, NT], I32)
        g.row_token = sb("row_token", [P, HT], U32)
        g.step_expert = sb("step_expert", [P, STEPS], I32)

        per_chunk = per_batch // DC

        def q_of(b, c):
            return g.pool[:, ds(b * per_batch + start + c * per_chunk, N)]

        def k_of(b, c):
            return g.pool[:, ds(b * per_batch + start + c * per_chunk + N, N)]

        def v_chunk(b, c):
            return g.pool[:, ds(b * per_batch + start + c * per_chunk + 2 * N, VT * P)].rearrange(
                "p (t d) -> p t d", d=P)

        def v_of(b, c, t, n):
            return g.pool[:, ds(b * per_batch + start + c * per_chunk + 2 * N + t * P, n * P)].rearrange(
                "p (t d) -> p t d", d=P)

        def w1_of(e):
            return g.pool[:, ds(e * per_expert, DC * F)].rearrange("p (c f) -> p c f", c=DC)

        def w2_of(e):
            return g.pool[:, ds(e * per_expert + DC * F, FC * D)].rearrange("p (m d) -> p m d", m=FC)

        g.q_of, g.k_of, g.v_of, g.v_chunk, g.w1_of, g.w2_of = q_of, k_of, v_of, v_chunk, w1_of, w2_of
        g.tick = ctx.enter_context(nc.semaphore("tick"))
        norm_project(nc, g)
        route(nc, g)
        attend(nc, g)
        experts(nc, g)
        combine(nc, g)


def lay_out(inputs):
    import numpy as np

    arrays = {name.split("_", 2)[2]: np.ascontiguousarray(a) for name, a in inputs.items()}
    arrays["bqk_cols"] = np.ascontiguousarray(arrays["bqkv"][:2 * D].reshape(2 * DC, P).T)
    arrays["b1_cols"] = np.ascontiguousarray(arrays["b1"].reshape(E * FC, P).T)
    return arrays


def kernel(**inputs):
    import concourse.bacc as bacc
    from concourse.bass_utils import run_bass_kernel_spmd

    nc = bacc.Bacc("TRN2", target_bir_lowering=False, num_devices=1)
    arrays = lay_out(inputs)
    g = Shared({
        name: nc.dram_tensor(f"in_{name}", a.shape, mybir.dt.from_np(a.dtype), kind="ExternalInput").ap()
        for name, a in arrays.items()})
    g.out = nc.dram_tensor("out", (B, N, D), F32, kind="ExternalOutput").ap()
    build(nc, g)
    run = run_bass_kernel_spmd(nc, [{f"in_{name}": a for name, a in arrays.items()}], core_ids=[0])
    return run.results[0]["out"]
```

```python
from contextlib import ExitStack

import concourse.bass as bass
from concourse import mybir
from concourse.alu_op_type import AluOpType as ALU

F32 = mybir.dt.float32
F32R = mybir.dt.float32r
I32 = mybir.dt.int32
U32 = mybir.dt.uint32
ACT = mybir.ActivationFunctionType
AX = mybir.AxisListType.X

P = 128
B, N, D = 8, 512, 256
T = B * N
H, DH = 16, 16
HALF = 64
E, F = 8, 1024
DC = D // P
FC = F // P
TB = N // P
NT = T // P
VT = TB + 1
HC = P // DH
ROWS = 2 * P
STEPS = (2 * T + E * (ROWS - 1)) // ROWS
RING = 3
assert STEPS % RING == 0
SLOTS = STEPS * ROWS
HT = SLOTS // P
EPS = 1e-5
FAR = 3.0e38
ds = bass.ds


class Shared:

    def __init__(self, inputs):
        self.x, self.Wqkv, self.bqkv, self.bqk_cols = (inputs[n] for n in ("x", "Wqkv", "bqkv", "bqk_cols"))
        self.Wout, self.bout = inputs["Wout"], inputs["bout"]
        self.router_w, self.router_b = inputs["router_w"], inputs["router_b"]
        self.w1, self.b1_cols, self.w2, self.b2 = (inputs[n] for n in ("w1", "b1_cols", "w2", "b2"))


START = 1


def start(eng, sems):
    for sem in sems:
        eng.sem_inc(sem, START)


def wait(eng, sem, count):
    eng.wait_ge(sem, count + START)


class Chain:

    def __init__(self, eng, sem, base=0):
        self.eng, self.sem, self.count, self.base = eng, sem, 0, base

    def add(self, ins, inc=1):
        ins.then_inc(self.sem, inc)
        self.count += inc
        return self

    def value(self):
        return self.base + self.count

    def wait(self):
        wait(self.eng, self.sem, self.value())


def wait_first(eng, sem, value, tick):
    wait(eng, sem, value)
    eng.sem_inc(tick, 1)


def norm_project(nc, g):
    with ExitStack() as ctx:
        def sb(name, shape, dt=F32):
            return ctx.enter_context(nc.sbuf_tensor(name, shape, dt))

        by = {"sp": [], "pool": [], "v": [], "act": [], "pe": []}

        def sem(name, engine):
            by[engine].append(ctx.enter_context(nc.semaphore(name)))
            return by[engine][-1]

        ps = ctx.enter_context(nc.psum_tensor("ps_project", [P, 8, 512], F32))
        w_raw = sb("w_raw", [P, DC, 3 * D])
        w_hi = sb("w_hi", [P, DC, 3 * D], F32R)
        w_lo = sb("w_lo", [P, DC, 3 * D], F32R)
        rw_raw = sb("rw_raw", [P, DC, E])
        rw = sb("rw", [P, DC, 2 * E], F32R)
        rb = sb("rb", [P, E])
        b_qk = sb("b_qk", [P, 2 * DC])
        b_v = sb("b_v", [P, D])
        x = sb("x_in", [P, 2, TB, D])
        xn = sb("xn", [P, 2, TB, D])
        stats = sb("stats", [P, TB, 6])
        mv = sb("mv", [P, TB, 2])
        var = sb("var", [P, TB])
        root = sb("root", [P, TB])
        rough = sb("rough", [P, TB])
        newton = sb("newton", [P, TB])
        rstd = sb("rstd", [P, TB])
        xt_hi = sb("xt_hi", [P, 2, DC, N + 2 * HALF], F32R)
        xt_lo = sb("xt_lo", [P, 2, DC, N + 2 * HALF], F32R)
        lg = sb("lg", [P, TB, E])

        s_w = sem("s_w", "sp")
        s_whi = sem("s_whi", "act")
        s_wlo = sem("s_wlo", "v")
        s_ident = sem("s_ident", "pool")
        s_x = sem("s_x", "sp")
        s_dve = sem("s_dve", "v")
        s_stats = sem("s_stats", "v")
        s_var = sem("s_var", "v")
        s_root = sem("s_root", "act")
        s_xn = sem("s_xn", "v")
        s_xnout = sem("s_xnout", "sp")
        s_tr = sem("s_tr", "pe")
        s_hi = sem("s_hi", "act")
        s_lo = sem("s_lo", "v")
        s_lg = sem("s_lg", "pe")
        s_lglo = sem("s_lglo", "v")
        s_lgout = sem("s_lgout", "v")
        s_qk = sem("s_qk", "pe")
        s_qout = sem("s_qout", "act")
        s_kout = sem("s_kout", "v")
        s_v = sem("s_v", "pe")
        s_vout = sem("s_vout", "v")
        s_pad = sem("s_pad", "v")

        bank_t, bank_l, bank_qk, bank_v = (0, 1), 2, (3, 4), (5, 6, 7)
        v_banks = [(0, 1), (2, 3), (4,)]
        x_rows = g.x.rearrange("b (t p) d -> b p t d", p=P)
        xn_rows = g.xn_dram.rearrange("(b t p) d -> b p t d", t=TB, p=P)

        with nc.Block() as block:
            @block.sync
            def _(sp):
                start(sp, by["sp"])

                def load(b, par):
                    sp.dma_start(x[:, par], x_rows[ds(b, 1)].rearrange("b p t d -> (b p) t d")
                                 ).then_inc(s_x, 16)

                load(0, 0)
                sp.dma_start(w_raw[:], g.Wqkv.rearrange("(c p) n -> p c n", p=P)).then_inc(s_w, 16)
                sp.dma_start(rw_raw[:], g.router_w.rearrange("(c p) e -> p c e", p=P)).then_inc(s_w, 16)
                sp.dma_start(rb[:], g.router_b.partition_broadcast(P)).then_inc(s_w, 16)
                sp.dma_start(b_qk[:], g.bqk_cols).then_inc(s_w, 16)
                sp.dma_start(b_v[:], g.bqkv[2 * D:3 * D].partition_broadcast(P)).then_inc(s_w, 16)

                wait(sp, s_x, 16)
                load(1, 1)
                with sp.Fori(0, B // 2) as pair:
                    for par in range(2):
                        b = 2 * pair + par
                        wait_first(sp, s_x, 16 * b + 32, g.tick)
                        wait_first(sp, s_xn, b + 1, g.tick)
                        load((b + 2) % B, par)
                        wait_first(sp, s_xnout, 16 * b, g.tick)
                        sp.dma_start(xn_rows[ds(b, 1)].rearrange("b p t d -> (b p) t d"),
                                     xn[:, par]).then_inc(s_xnout, 16)
                wait(sp, s_xnout, 16 * B)
                wait(sp, s_x, 16 * (B + 2))

            @block.gpsimd
            def _(pool):
                start(pool, by["pool"])
                pool.memset(g.ident[:], 0.0).then_inc(s_ident, 1)
                wait(pool, s_ident, 1)
                pool.affine_select(out=g.ident[:], in_=g.ident[:], compare_op=ALU.not_equal, fill=1.0,
                                   base=0, pattern=[[-1, P]], channel_multiplier=1).then_inc(s_ident, 1)

            @block.vector
            def _(v):
                start(v, by["v"])
                for buf in (xt_hi, xt_lo):
                    for par in range(2):
                        for c in range(DC):
                            v.memset(buf[:, par, c, 0:HALF].bitcast(F32), 0.0).then_inc(s_pad, 1)
                            v.memset(buf[:, par, c, N + HALF:N + 2 * HALF].bitcast(F32), 0.0).then_inc(s_pad, 1)

                def statistics(b, ring):
                    chain = Chain(v, s_stats, 2 * b)
                    wait(v, s_x, 16 * b + 16)
                    for t in range(TB):
                        ins = v.bn_stats(stats[:, t, :], x[:, ring, t, :])
                    chain.add(ins)
                    wait_first(v, s_stats, chain.value(), g.tick)
                    for t in range(TB):
                        ins = v.bn_aggr(mv[:, t, :], stats[:, t, :])
                    chain.add(ins).wait()
                    v.tensor_scalar(var[:], mv[:, :, 1], EPS, None, ALU.add).then_inc(s_var, 1)

                def norm(b, ring, fresh=False):
                    chain = Chain(v, s_dve, 5 * b)
                    wait(v, s_root, b + 1)
                    chain.add(v.reciprocal(rough[:], root[:])).wait()
                    chain.add(v.tensor_tensor(newton[:], rough[:], rough[:], ALU.mult)).wait()
                    chain.add(v.tensor_tensor(newton[:], newton[:], var[:], ALU.mult)).wait()
                    chain.add(v.tensor_scalar(newton[:], newton[:], -0.5, 1.5, ALU.mult, ALU.add)).wait()
                    chain.add(v.tensor_tensor(rstd[:], rough[:], newton[:], ALU.mult)).wait()
                    if not fresh:
                        wait(v, s_tr, 2 * b)
                        wait(v, s_xnout, 16 * b - 16)
                    for t in range(TB):
                        ins = v.tensor_scalar(xn[:, ring, t, :], x[:, ring, t, :], mv[:, t, 0:1],
                                              rstd[:, t:t + 1], ALU.subtract, ALU.mult)
                    ins.then_inc(s_xn, 1)

                def lo_of_tokens(b, ring):
                    for c in range(DC):
                        wait(v, s_hi, 2 * b + c + 1)
                        v.tensor_tensor(xt_lo[:, ring, c, HALF:HALF + N], ps[:, bank_t[c], :],
                                        xt_hi[:, ring, c, HALF:HALF + N].bitcast(F32),
                                        ALU.subtract).then_inc(s_lo, 1)

                statistics(0, 0)
                norm(0, 0, True)
                wait(v, s_whi, 2)
                v.tensor_tensor(w_lo[:], w_raw[:], w_hi[:].bitcast(F32), ALU.subtract).then_inc(s_wlo, 1)
                v.tensor_tensor(rw[:, :, E:2 * E], rw_raw[:], rw[:, :, 0:E].bitcast(F32),
                                ALU.subtract).then_inc(s_wlo, 1)
                lo_of_tokens(0, 0)
                statistics(1, 1)
                with v.Fori(0, B // 2) as pair:
                    for par in range(2):
                        b = 2 * pair + par
                        norm(b + 1, 1 - par)
                        for m in (2, 3):
                            wait(v, s_qk, 4 * b + m + 1)
                            v.tensor_scalar(g.k_of(b, m - 2), ps[:, bank_qk[m % 2], :], b_qk[:, m:m + 1],
                                            None, ALU.add).then_inc(s_kout, 1)
                        statistics(b + 2, par)
                        lo_of_tokens(b + 1, 1 - par)
                        wait(v, s_lg, b + 1)
                        lg_ps = ps[:, bank_l, 0:TB * 2 * E].rearrange("p (t e) -> p t e", t=TB)
                        v.tensor_tensor(lg[:], lg_ps[:, :, E:2 * E],
                                        rb[:].unsqueeze(1).to_broadcast([P, TB, E]), ALU.add
                                        ).then_inc(s_lglo, 1)
                        wait(v, s_lglo, b + 1)
                        v.tensor_tensor(g.logits[:, ds(b * TB, TB), :], lg_ps[:, :, 0:E], lg[:], ALU.add
                                        ).then_inc(s_lgout, 1)
                        for n, tiles in enumerate(v_banks):
                            wait(v, s_v, 3 * b + n + 1)
                            tiles_ps = ps[:, bank_v[n], 0:D * len(tiles)].rearrange("p (t d) -> p t d", d=D)
                            for c in range(DC):
                                ins = v.tensor_tensor(
                                    g.v_of(b, c, tiles[0], len(tiles)), tiles_ps[:, :, c * P:(c + 1) * P],
                                    b_v[:, c * P:(c + 1) * P].unsqueeze(1).to_broadcast([P, len(tiles), P]),
                                    ALU.add)
                            ins.then_inc(s_vout, 1)
                wait(v, s_vout, 3 * B)

            @block.scalar
            def _(act):
                start(act, by["act"])

                def variance_root(b):
                    wait(act, s_var, b + 1)
                    act.activation(root[:], var[:], ACT.Sqrt).then_inc(s_root, 1)

                def hi_of_tokens(b, ring):
                    for c in range(DC):
                        wait(act, s_tr, 2 * b + c + 1)
                        act.activation(xt_hi[:, ring, c, HALF:HALF + N], ps[:, bank_t[c], :],
                                       ACT.Copy).then_inc(s_hi, 1)

                variance_root(0)
                wait(act, s_w, 80)
                act.activation(w_hi[:], w_raw[:], ACT.Copy).then_inc(s_whi, 1)
                act.activation(rw[:, :, 0:E], rw_raw[:], ACT.Copy).then_inc(s_whi, 1)
                hi_of_tokens(0, 0)
                variance_root(1)
                with act.Fori(0, B // 2) as pair:
                    for par in range(2):
                        b = 2 * pair + par
                        for m in (0, 1):
                            wait(act, s_qk, 4 * b + m + 1)
                            act.activation(g.q_of(b, m), ps[:, bank_qk[m % 2], :], ACT.Identity,
                                           bias=b_qk[:, m:m + 1]).then_inc(s_qout, 1)
                        hi_of_tokens(b + 1, 1 - par)
                        variance_root(b + 2)

            @block.tensor
            def _(pe):
                start(pe, by["pe"])
                wait(pe, s_ident, 2)

                def transpose_tokens(b, ring):
                    wait(pe, s_xn, b + 1)
                    for c in range(DC):
                        for t in range(TB):
                            ins = pe.transpose(ps[:, bank_t[c], t * P:(t + 1) * P],
                                               xn[:, ring, t, c * P:(c + 1) * P], g.ident[:])
                        ins.then_inc(s_tr, 1)

                transpose_tokens(0, 0)
                wait(pe, s_wlo, 2)
                wait(pe, s_pad, 16)
                with pe.Fori(0, B // 2) as pair:
                    for par in range(2):
                        b = 2 * pair + par
                        hi, lo = xt_hi[:, par], xt_lo[:, par]
                        wait(pe, s_lo, 2 * b + 2)
                        for m in range(4):
                            if m < 2:
                                wait(pe, s_kout, 2 * b)
                            else:
                                wait(pe, s_qout, 2 * b + m - 1)
                            n = 0
                            for c in range(DC):
                                for w, xx in ((w_hi, hi), (w_hi, lo), (w_lo, hi)):
                                    ins = pe.matmul(ps[:, bank_qk[m % 2], :], w[:, c, m * P:(m + 1) * P],
                                                    xx[:, c, HALF:HALF + N], start=(n == 0), stop=(n == 5))
                                    n += 1
                            ins.then_inc(s_qk, 1)
                        transpose_tokens(b + 1, 1 - par)
                        wait(pe, s_lgout, b)
                        for t in range(TB):
                            n = 0
                            for c in range(DC):
                                for xx in (hi, lo):
                                    ins = pe.matmul(ps[:, bank_l, t * 2 * E:(t + 1) * 2 * E],
                                                    xx[:, c, HALF + t * P:HALF + (t + 1) * P], rw[:, c, :],
                                                    start=(n == 0), stop=(n == 3))
                                    n += 1
                        ins.then_inc(s_lg, 1)
                        for nb, tiles in enumerate(v_banks):
                            wait(pe, s_vout, 3 * b)
                            for j, t in enumerate(tiles):
                                n = 0
                                for c in range(DC):
                                    for xx, w in ((hi, w_hi), (lo, w_hi), (hi, w_lo)):
                                        ins = pe.matmul(ps[:, bank_v[nb], j * D:(j + 1) * D],
                                                        xx[:, c, t * P:(t + 1) * P], w[:, c, 2 * D:3 * D],
                                                        start=(n == 0), stop=(n == 5))
                                        n += 1
                            ins.then_inc(s_v, 1)


def route(nc, g):
    with ExitStack() as ctx:
        def sb(name, shape, dt=F32):
            return ctx.enter_context(nc.sbuf_tensor(name, shape, dt))

        by = {"sp": [], "pool": [], "v": [], "act": [], "pe": []}

        def sem(name, engine):
            by[engine].append(ctx.enter_context(nc.semaphore(name)))
            return by[engine][-1]

        ps = ctx.enter_context(nc.psum_tensor("ps_route", [P, 4, 512], F32))
        before = sb("before", [P, P])
        ones = sb("ones", [P, P])
        expert_rank = sb("expert_rank", [P, E])
        step_iota = sb("step_iota", [P, STEPS])
        token = sb("token", [P, NT])
        plain = sb("plain", [P, HT, 2], I32)
        top = sb("top", [P, 2, NT])
        pick = sb("pick", [P, 2, NT, E])
        rest = sb("rest", [P, NT, E])
        tied = sb("tied", [P, NT, E])
        win = sb("win", [P, NT])
        both = sb("both", [P, NT, E])
        ratio = sb("ratio", [P, NT])
        denom = sb("denom", [P, NT])
        gate = sb("gate", [P, 2, NT])
        weighted = sb("weighted", [P, 2, NT, E])
        in_tile = sb("in_tile", [P, NT, E])
        count = sb("count", [P, E, NT])
        through = sb("through", [P, E, NT])
        earlier = sb("earlier", [P, NT, E])
        others = sb("others", [P, NT, E])
        rank = sb("rank", [P, NT, E])
        number = sb("number", [P, E])
        total_i = sb("total_i", [P, E], I32)
        steps_i = sb("steps_i", [P, E], I32)
        steps = sb("steps", [P, E])
        steps_end = sb("steps_end", [P, E])
        first_row = sb("first_row", [P, E])
        end_row = sb("end_row", [P, E])
        passed = sb("passed", [P, STEPS, E])
        expert_f = sb("expert_f", [P, STEPS])
        beyond = sb("beyond", [P, NT, E])
        row_i = sb("row_i", [P, NT, E], I32)
        part_i = sb("part_i", [P, 2, NT, E], I32)
        part = sb("part", [P, 2, NT, E])

        s_c = sem("s_c", "pool")
        s_v = sem("s_v2", "v")
        s_pick = sem("s_pick", "v")
        s_count = sem("s_count", "pe")
        s_gap = sem("s_gap", "v")
        s_exp = sem("s_exp", "act")
        s_plain = sem("s_plain", "v")
        s_table = sem("s_table", "sp")

        with nc.Block() as block:
            @block.sync
            def _(sp):
                start(sp, by["sp"])
                wait(sp, s_plain, 2)
                sp.dma_start(g.table_dram.rearrange("(p h) w -> p h w", p=P), plain[:].bitcast(F32)
                             ).then_inc(s_table, 16)
                wait(sp, s_table, 16)

            @block.gpsimd
            def _(pool):
                start(pool, by["pool"])
                pool.memset(ones[:], 1.0).then_inc(s_c, 1)
                pool.memset(before[:], 1.0).then_inc(s_c, 1)
                pool.iota(expert_rank[:], [[-1, E]], base=E, channel_multiplier=0,
                          allow_small_or_imprecise_dtypes=True).then_inc(s_c, 1)
                pool.iota(step_iota[:], [[1, STEPS]], base=0, channel_multiplier=0,
                          allow_small_or_imprecise_dtypes=True).then_inc(s_c, 1)
                pool.iota(token[:], [[P, NT]], base=0, channel_multiplier=1,
                          allow_small_or_imprecise_dtypes=True).then_inc(s_c, 1)
                pool.iota(plain[:], [[P, HT], [0, 2]], base=0, channel_multiplier=1).then_inc(s_c, 1)
                wait(pool, s_c, 6)
                pool.affine_select(out=before[:], in_=before[:], compare_op=ALU.is_gt, fill=0.0, base=0,
                                   pattern=[[1, P]], channel_multiplier=-1).then_inc(s_c, 1)

            @block.vector
            def _(v):
                start(v, by["v"])
                chain = Chain(v, s_v)

                def do(ins):
                    chain.add(ins).wait()

                def per_tile(a):
                    return a.unsqueeze(2).to_broadcast([P, NT, E])

                def per_expert(a):
                    return a.unsqueeze(1).to_broadcast([P, NT, E])

                wait(v, s_c, 7)
                order = per_expert(expert_rank[:])
                for n in range(2):
                    left = g.logits if n == 0 else rest[:]
                    do(v.tensor_reduce(top[:, n, :], left, AX, ALU.max))
                    do(v.tensor_tensor(tied[:], left, per_tile(top[:, n, :]), ALU.is_equal))
                    do(v.tensor_tensor(tied[:], tied[:], order, ALU.mult))
                    do(v.tensor_reduce(win[:], tied[:], AX, ALU.max))
                    do(v.tensor_tensor(pick[:, n], order, per_tile(win[:]), ALU.is_equal))
                    if n == 0:
                        do(v.scalar_tensor_tensor(out=rest[:], in0=pick[:, 0], scalar=-FAR, in1=left,
                                                  op0=ALU.mult, op1=ALU.add))
                v.tensor_tensor(ratio[:], top[:, 1, :], top[:, 0, :], ALU.subtract).then_inc(s_gap, 1)
                v.tensor_tensor(both[:], pick[:, 0], pick[:, 1], ALU.add).then_inc(s_pick, 1)
                v.tensor_scalar(plain[:, :, 0], plain[:, :, 0], T - 1, None, ALU.bitwise_and).then_inc(s_plain, 1)
                v.memset(plain[:, :, 1], 0).then_inc(s_plain, 1)
                wait(v, s_exp, 1)
                do(v.tensor_scalar(denom[:], ratio[:], 1.0, None, ALU.add))
                do(v.reciprocal(gate[:, 0, :], denom[:]))
                do(v.tensor_tensor(gate[:, 1, :], ratio[:], gate[:, 0, :], ALU.mult))
                do(v.tensor_tensor(weighted[:].rearrange("p n t e -> p (n t) e"),
                                   pick[:].rearrange("p n t e -> p (n t) e"),
                                   gate[:].rearrange("p n t -> p (n t)").unsqueeze(2).to_broadcast([P, 2 * NT, E]),
                                   ALU.mult))
                v.tensor_tensor(g.entry[:, :, :, 1], weighted[:, 0], weighted[:, 1], ALU.add)
                v.tensor_copy(g.entry[:, :, :, 0].bitcast(I32), per_tile(token[:]))
                wait(v, s_count, 2)
                v.tensor_copy(in_tile[:], ps[:, 0, 0:NT * E].rearrange("p (t e) -> p t e", e=E))
                do(v.tensor_copy(count[:], ps[:, 1, 0:NT * E].rearrange("p (t e) -> p e t", e=E)))
                for e in range(E):
                    ins = v.tensor_tensor_scan(through[:, e, :], ones[:, 0:NT], count[:, e, :], 0.0,
                                               ALU.mult, ALU.add)
                do(ins)
                v.tensor_copy(number[:], through[:, :, NT - 1])
                do(v.tensor_scalar(total_i[:], through[:, :, NT - 1], float(ROWS - 1), None, ALU.add))
                do(v.tensor_scalar(steps_i[:], total_i[:], ROWS.bit_length() - 1, None,
                                   ALU.arith_shift_right))
                do(v.tensor_copy(steps[:], steps_i[:]))
                do(v.tensor_tensor_scan(steps_end[:], ones[:, 0:E], steps[:], 0.0, ALU.mult, ALU.add))
                v.tensor_scalar(end_row[:], steps_end[:], float(ROWS), None, ALU.mult)
                do(v.tensor_tensor(first_row[:], steps_end[:], steps[:], ALU.subtract))
                do(v.tensor_scalar(first_row[:], first_row[:], float(ROWS), None, ALU.mult))
                do(v.tensor_tensor(through[:], through[:], count[:], ALU.subtract))
                do(v.tensor_tensor(earlier[:], in_tile[:], through[:].rearrange("p e t -> p t e"), ALU.add))
                do(v.tensor_tensor(others[:], per_tile(token[:]), earlier[:], ALU.subtract))
                do(v.tensor_tensor(others[:], others[:], per_expert(number[:]), ALU.add))
                do(v.tensor_tensor(rank[:], earlier[:], others[:], ALU.subtract))
                do(v.tensor_tensor(rank[:], rank[:], both[:], ALU.mult))
                do(v.tensor_tensor(rank[:], rank[:], others[:], ALU.add))
                do(v.tensor_tensor(rank[:], rank[:], per_expert(first_row[:]), ALU.add))
                v.tensor_tensor(beyond[:], rank[:], per_expert(end_row[:]), ALU.is_ge)
                do(v.tensor_copy(row_i[:], rank[:]))
                v.tensor_scalar(part_i[:, 0], row_i[:], P.bit_length() - 1, None, ALU.arith_shift_right)
                do(v.tensor_scalar(part_i[:, 1], row_i[:], P - 1, None, ALU.bitwise_and))
                do(v.tensor_copy(part[:], part_i[:]))
                do(v.scalar_tensor_tensor(out=rank[:], in0=part[:, 1], scalar=float(HT), in1=part[:, 0],
                                          op0=ALU.mult, op1=ALU.add))
                do(v.scalar_tensor_tensor(out=g.entry_at[:], in0=beyond[:], scalar=float(SLOTS), in1=rank[:],
                                          op0=ALU.mult, op1=ALU.add))
                do(v.tensor_tensor(passed[:], step_iota[:].unsqueeze(2).to_broadcast([P, STEPS, E]),
                                   steps_end[:].unsqueeze(1).to_broadcast([P, STEPS, E]), ALU.is_ge))
                do(v.tensor_reduce(expert_f[:], passed[:], AX, ALU.add))
                do(v.tensor_scalar(g.step_expert[:], expert_f[:], float(E - 1), None, ALU.min))

            @block.scalar
            def _(act):
                start(act, by["act"])
                wait(act, s_gap, 1)
                act.activation(ratio[:], ratio[:], ACT.Exp).then_inc(s_exp, 1)

            @block.tensor
            def _(pe):
                start(pe, by["pe"])
                wait(pe, s_c, 7)
                wait(pe, s_pick, 1)
                sel = both[:].rearrange("p t e -> p (t e)")
                pe.matmul(ps[:, 0, 0:NT * E], before[:], sel, start=True, stop=True).then_inc(s_count, 1)
                pe.matmul(ps[:, 1, 0:NT * E], ones[:], sel, start=True, stop=True).then_inc(s_count, 1)


def attend(nc, g):
    with ExitStack() as ctx:
        def sb(name, shape, dt=F32):
            return ctx.enter_context(nc.sbuf_tensor(name, shape, dt))

        by = {"sp": [], "pool": [], "v": [], "act": [], "pe": []}

        def sem(name, engine):
            by[engine].append(ctx.enter_context(nc.semaphore(name)))
            return by[engine][-1]

        W = 2 * P
        ps = ctx.enter_context(nc.psum_tensor("ps_attend", [P, 8, 512], F32))
        wo_hi = sb("wo_hi", [P, DC, D], F32R)
        wo_lo = sb("wo_lo", [P, DC, D], F32R)
        b_o = sb("b_o", [P, D])
        band = sb("band", [P, W])
        head_rows = sb("head_rows", [P, HC])
        q_s = sb("q_s", [P, 2, N], F32R)
        k_s = sb("k_s", [P, 2, 2, N], F32R)
        v_s = sb("v_s", [P, 2, VT, P], F32R)
        q_m = sb("q_m", [P, 2, 2, N], F32R)
        v_m = sb("v_m", [P, 2, 2, VT, P], F32R)
        wo_raw = g.w2_of(0)[:, 0:DC, :]
        wt = g.pool[:, 0:2 * TB * W].rearrange("p (r t w) -> p r t w", r=2, t=TB)
        low = sb("low", [P, 2, TB])
        total = sb("total", [P, DC, TB, HC])
        inv_s = sb("inv_s", [P, TB, HC])
        inv = sb("inv", [P, TB, HC, DH])
        inv_t = sb("inv_t", [P, N])
        pt = sb("pt", [P, 2, 2, 2, N], F32R)
        a_hi = sb("a_hi", [P, DC, N], F32R)
        a_lo = sb("a_lo", [P, DC, N], F32R)
        xb = sb("xb", [P, TB, D])
        entry = sb("entry_b", [P, TB * E, 2])
        entry_at = sb("entry_at_b", [P, TB * E], U32)

        s_in = sem("s_in", "sp")
        s_const = sem("s_const", "pool")
        s_wohi = sem("s_wohi", "act")
        s_wolo = sem("s_wolo", "v")
        s_xb = sem("s_xb", "sp")
        s_out = sem("s_out", "sp")
        s_wload = sem("s_wload", "sp")
        s_qhi = sem("s_qhi", "act")
        s_qlo = sem("s_qlo", "v")
        s_khi = sem("s_khi", "act")
        s_klo = sem("s_klo", "pool")
        s_vhi = sem("s_vhi", "act")
        s_vlo = sem("s_vlo", "v")
        s_qm = sem("s_qm", "v")
        s_vz = sem("s_vz", "pool")
        s_vm = sem("s_vm", "pool")
        s_s = sem("s_s", "pe")
        s_low = sem("s_low", "v")
        s_exp = sem("s_exp3", "act")
        s_t = sem("s_t", "pe")
        s_phi = sem("s_phi", "act")
        s_plo = sem("s_plo", "v")
        s_pv = sem("s_pv", "pe")
        s_rec = sem("s_rec", "v")
        s_inv = sem("s_inv", "v")
        s_invt = sem("s_invt", "pe")
        s_invs = sem("s_invs", "act")
        s_a = sem("s_a", "v")
        s_ahi = sem("s_ahi", "act")
        s_alo = sem("s_alo", "v")
        s_proj = sem("s_proj", "pe")
        s_done = sem("s_done", "v")
        s_biased = sem("s_biased", "pool")
        s_entry = sem("s_entry", "pool")
        s_rows = sem("s_rows", "sp")
        s_sent = [[ctx.enter_context(nc.semaphore(f"s_sent{r}{j}")) for j in range(2)] for r in range(2)]

        bank_s, bank_t, bank_o, bank_m = ((0, 1), (2, 3)), (4, 5), 6, 7
        heads = DC * HC
        LAG = 2
        x_rows = g.x.rearrange("b (t p) d -> b p t d", p=P)
        out_rows = g.out.rearrange("b (t p) d -> b p t d", p=P)

        def window(i):
            begin = max(0, HALF - P * i)
            end = min(W, N + HALF - P * i)
            return begin, end, begin + P * i - HALF

        def chunk_of(b, k):
            c = k // HC
            return (b, c) if c < DC else ((b + 1) % B | b // (B - 1) * (B - 1), c - DC)

        def each_batch(eng, batch):
            batch(0, True)
            with eng.Fori(1, B) as b:
                batch(b, False)

        with nc.Block() as block:
            @block.sync
            def _(sp):
                start(sp, by["sp"])
                sp.dma_start(wo_raw, g.Wout.rearrange("(c p) n -> p c n", p=P)).then_inc(s_in, 16)
                sp.dma_start(b_o[:], g.bout.partition_broadcast(P)).then_inc(s_in, 16)

                def load_w1(e):
                    sp.dma_start(g.w1_of(e), g.w1[ds(e, 1)].rearrange("e (c p) f -> (e p) c f", p=P)
                                 ).then_inc(s_wload, 16)

                def batch(b, first, last=False):
                    if not first:
                        wait_first(sp, s_out, 16 * b, g.tick)
                    sp.dma_start(xb[:], x_rows[ds(b, 1)].rearrange("b p t d -> (b p) t d")).then_inc(s_xb, 16)
                    wait_first(sp, s_vlo, 2 * b + 2, g.tick)
                    for split in (s_qlo, s_klo, s_vhi):
                        wait_first(sp, split, 2 * b + 3, g.tick)
                    if not first:
                        wait_first(sp, s_wload, 32 * b - 16, g.tick)
                    if not (first or last):
                        load_w1(b)
                    if not last:
                        sp.dma_start(g.w2_of(b), g.w2[ds(b, 1)].rearrange("e (m p) d -> (e p) m d", p=P)
                                     ).then_inc(s_wload, 16)
                    if last:
                        wait(sp, s_t, 2 * heads * B)
                        wait(sp, s_low, 2 * (heads * B + 2))
                        load_w1(0)
                        for j in range(4):
                            sp.wait_ge(s_sent[j // 2][j % 2], 16 * B * HC)
                        sp.dma_start(g.rows[:], g.table_dram.rearrange("(p h) w -> p h w", p=P)
                                     ).then_inc(s_rows, 16)
                    wait_first(sp, s_done, 2 * b + 2, g.tick)
                    sp.dma_start(out_rows[ds(b, 1)].rearrange("b p t d -> (b p) t d"), xb[:]).then_inc(s_out, 16)

                batch(0, True)
                with sp.Fori(1, B - 1) as b:
                    batch(b, False)
                batch(B - 1, False, True)
                wait(sp, s_rows, 16)
                wait(sp, s_out, 16 * B)
                wait(sp, s_wload, 32 * (E - 1))

            @block.gpsimd
            def _(pool):
                start(pool, by["pool"])
                pool.memset(band[:], 0.0).then_inc(s_vz, 1)
                pool.memset(head_rows[:], 1.0).then_inc(s_vz, 1)
                wait(pool, s_vz, 2)
                pool.affine_select(out=band[:], in_=band[:], compare_op=ALU.is_ge, fill=FAR, base=0,
                                   pattern=[[1, W]], channel_multiplier=-1).then_inc(s_vz, 1)
                pool.affine_select(out=head_rows[:], in_=head_rows[:], compare_op=ALU.is_ge, fill=0.0,
                                   base=0, pattern=[[-DH, HC]], channel_multiplier=1).then_inc(s_vz, 1)
                wait(pool, s_vz, 4)
                pool.affine_select(out=band[:], in_=band[:], compare_op=ALU.is_ge, fill=FAR, base=2 * HALF,
                                   pattern=[[-1, W]], channel_multiplier=1).then_inc(s_const, 1)
                pool.affine_select(out=head_rows[:], in_=head_rows[:], compare_op=ALU.is_ge, fill=0.0,
                                   base=DH - 1, pattern=[[DH, HC]], channel_multiplier=-1).then_inc(s_const, 1)
                wait(pool, s_khi, 1)
                pool.tensor_tensor(k_s[:, 0, 1], g.k_of(0, 0), k_s[:, 0, 0].bitcast(F32), ALU.subtract
                                   ).then_inc(s_klo, 1)
                for ring in range(2):
                    pool.memset(v_m[:, ring].bitcast(F32), 0.0).then_inc(s_const, 1)
                pool.memset(wt[:, :, 0, 0:HALF], 0.0).then_inc(s_const, 1)
                pool.memset(wt[:, :, TB - 1, W - HALF:W], 0.0).then_inc(s_const, 1)
                wait(pool, s_const, 6)

                def send(b, n, first=False):
                    if not (first and n < LAG + 2):
                        for j in range(2):
                            pool.wait_ge(s_sent[n % 2][j], 16 * (HC * b + n // 2 - LAG // 2))
                            pool.sem_inc(g.tick, 1)
                    if n == LAG:
                        if not first:
                            for j in range(2):
                                pool.wait_ge(s_sent[1][j], 16 * HC * b)
                                pool.sem_inc(g.tick, 1)
                        tiles = ds(b * TB * E, TB * E)
                        pool.tensor_copy(entry[:], g.entry[:].rearrange("p t e w -> p (t e) w")[:, tiles, :]
                                         ).then_inc(s_entry, 1)
                        pool.tensor_copy(entry_at[:], g.entry_at[:].rearrange("p t e -> p (t e)")[:, tiles]
                                         ).then_inc(s_entry, 1)
                        wait_first(pool, s_entry, 2 * b + 2, g.tick)
                    for j in range(2):
                        at = 2 * ((n - LAG) % heads) + j
                        pool.indirect_dma_start(
                            g.table_dram, bass.IndirectOffsetOnAxis(ap=entry_at[:, at:at + 1], axis=0),
                            entry[:, at, :], None, bounds_check=SLOTS - 1, oob_is_err=False
                            ).then_inc(s_sent[n % 2][j], 16)

                def batch(b, first):
                    for n in range(heads):
                        m, j, ring = heads * b + n, n % HC, n % 2
                        if j == 0:
                            wait_first(pool, s_vlo, 2 * b + n // HC + 1, g.tick)
                        if not (first and n < 2):
                            wait_first(pool, s_pv, m - 1, g.tick)
                        old = DH * ((j - 2) % HC)
                        pool.memset(v_m[:, ring, :, :, old:old + DH].rearrange("p h t d -> p (h t) d").bitcast(F32), 0.0)
                        pool.tensor_copy(v_m[:, ring, :, :, DH * j:DH * (j + 1)].rearrange("p h t d -> p (h t) d"),
                                         v_s[:, :, :, DH * j:DH * (j + 1)].rearrange("p h t d -> p (h t) d")
                                         ).then_inc(s_vm, 1)
                        if not (first and n < LAG):
                            send(b, n, first)
                        if n % HC == HC - 4:
                            src, c = chunk_of(b, n + 4)
                            wait_first(pool, s_khi, 2 * b + n // HC + 2, g.tick)
                            pool.tensor_tensor(k_s[:, c, 1], g.k_of(src, c), k_s[:, c, 0].bitcast(F32),
                                               ALU.subtract).then_inc(s_klo, 1)
                        if n == 9:
                            wait_first(pool, s_xb, 16 * b + 16, g.tick)
                        if 9 <= n < 9 + TB:
                            ins = pool.tensor_tensor(xb[:, n - 9], xb[:, n - 9], b_o[:], ALU.add)
                        if n == 8 + TB:
                            ins.then_inc(s_biased, 1)

                each_batch(pool, batch)
                for n in range(LAG):
                    send(B, n)

            @block.vector
            def _(v):
                start(v, by["v"])

                def lo_of_q(b, k):
                    u, (src, c) = 2 * b + k // HC, chunk_of(b, k)
                    wait(v, s_qhi, u + 1)
                    v.scalar_tensor_tensor(out=q_s[:, 1], in0=g.q_of(src, c), scalar=-DH ** -0.5,
                                           in1=q_s[:, 0].bitcast(F32), op0=ALU.mult, op1=ALU.subtract
                                           ).then_inc(s_qlo, 1)

                def lo_of_values(b, k):
                    u, (src, c) = 2 * b + k // HC, chunk_of(b, k)
                    wait(v, s_vhi, u + 1)
                    v.tensor_tensor(v_s[:, 1], g.v_chunk(src, c), v_s[:, 0].bitcast(F32), ALU.subtract
                                    ).then_inc(s_vlo, 1)

                def one_head(b, k, fresh=False):
                    m, j, ring = heads * b + k, k % HC, k % 2
                    if not fresh:
                        wait(v, s_s, m - 1)
                    if j == 0:
                        wait(v, s_qlo, 2 * b + k // HC + 1)
                    v.tensor_scalar(q_m[:, ring], q_s[:].bitcast(F32), head_rows[:, j:j + 1], None,
                                    ALU.mult).then_inc(s_qm, 1)

                def mask(b, k, fresh=False):
                    m, ring = heads * b + k, k % 2
                    wait(v, s_s, m + 1)
                    if not fresh:
                        wait_first(v, s_t, 2 * m - 2, g.tick)
                    for i in range(TB):
                        f, l, _ = window(i)
                        bank = bank_s[ring][i // 2]
                        ins = v.tensor_tensor_reduce(
                            out=wt[:, ring, i, f:l], in0=ps[:, bank, W * (i % 2) + f:W * (i % 2) + l],
                            in1=band[:, f:l], scale=1.0, scalar=FAR, op0=ALU.add, op1=ALU.min,
                            accum_out=low[:, ring, i:i + 1])
                        if i % 2:
                            ins.then_inc(s_low, 1)

                def lo_of_weights(b, k):
                    m, (hi, lo) = heads * b + k, (pt[:, k % 2, 0], pt[:, k % 2, 1])
                    for h in range(2):
                        wait(v, s_phi, 2 * m + h + 1)
                        v.tensor_tensor(lo[:, h], ps[:, bank_t[h], :], hi[:, h].bitcast(F32),
                                        ALU.subtract).then_inc(s_plo, 1)

                def invert(b, c):
                    u = 2 * b + c
                    wait(v, s_exp, heads * b + HC * (c + 1))
                    v.reciprocal(inv_s[:], total[:, c]).then_inc(s_rec, 1)
                    wait(v, s_rec, u + 1)
                    v.tensor_copy(inv[:], inv_s[:].unsqueeze(3).to_broadcast([P, TB, HC, DH])).then_inc(s_inv, 1)

                def normalise(u):
                    wait(v, s_pv, HC * (u + 1))
                    wait(v, s_invs, u + 1)
                    v.tensor_tensor(inv_t[:], ps[:, bank_o, :], inv_t[:], ALU.mult).then_inc(s_a, 1)

                def lo_of_output(u, c):
                    wait(v, s_ahi, u + 1)
                    v.tensor_tensor(a_lo[:, c], inv_t[:], a_hi[:, c].bitcast(F32), ALU.subtract).then_inc(s_alo, 1)

                def add_projected(b, h, bank=bank_m):
                    wait(v, s_biased, b + 1)
                    wait(v, s_proj, 2 * b + h + 1)
                    v.tensor_tensor(xb[:, 2 * h:2 * h + 2], ps[:, bank, :].rearrange("p (t d) -> p t d", d=D),
                                    xb[:, 2 * h:2 * h + 2], ALU.add).then_inc(s_done, 1)

                lo_of_q(0, 0)
                wait(v, s_const, 2)
                one_head(0, 0, True)
                one_head(0, 1, True)
                mask(0, 0, True)
                one_head(0, 2)
                mask(0, 1, True)

                def batch(b, first):
                    for n in range(heads):
                        if n % HC == 0:
                            lo_of_values(b, n)
                        if n % HC == HC - 3:
                            lo_of_q(b, n + 3)
                        one_head(b, n + 3)
                        lo_of_weights(b, n)
                        mask(b, n + 2)
                        if n % HC == 0 and not (first and n == 0):
                            normalise(2 * b + n // HC - 1)
                        if n % HC == 1 and not (first and n == 1):
                            lo_of_output(2 * b + n // HC - 1, (n // HC - 1) % DC)
                        if first and n == 3:
                            wait(v, s_wohi, 1)
                            v.tensor_tensor(wo_lo[:], wo_raw, wo_hi[:].bitcast(F32), ALU.subtract
                                            ).then_inc(s_wolo, 1)
                        if n in (3, 5) and not first:
                            add_projected(b - 1, (n - 3) // 2)
                        if n % HC == HC - 1:
                            invert(b, n // HC)

                each_batch(v, batch)
                normalise(2 * B - 1)
                lo_of_output(2 * B - 1, DC - 1)
                add_projected(B - 1, 0)
                add_projected(B - 1, 1, bank_t[0])

            @block.scalar
            def _(act):
                start(act, by["act"])

                def hi_of_q(b, k):
                    src, c = chunk_of(b, k)
                    if k:
                        wait_first(act, s_qm, heads * b + k, g.tick)
                    act.activation(q_s[:, 0], g.q_of(src, c), ACT.Copy, scale=-DH ** -0.5).then_inc(s_qhi, 1)

                def hi_of_k(b, k):
                    src, c = chunk_of(b, k)
                    if k:
                        wait_first(act, s_s, heads * b + k - HC, g.tick)
                    act.activation(k_s[:, c, 0], g.k_of(src, c), ACT.Copy).then_inc(s_khi, 1)

                def hi_of_values(b, k):
                    src, c = chunk_of(b, k)
                    if k:
                        wait_first(act, s_vm, heads * b + k, g.tick)
                    act.activation(v_s[:, 0], g.v_chunk(src, c), ACT.Copy).then_inc(s_vhi, 1)

                def exponentials(b, k, half):
                    m, c, j, ring = heads * b + k, k // HC % DC, k % HC, k % 2
                    if j == 0 and half == 0 and k:
                        wait(act, s_inv, 2 * b + k // HC - 1)
                    wait(act, s_low, 2 * m + half + 1)
                    for i in (2 * half, 2 * half + 1):
                        f, l, _ = window(i)
                        ins = act.activation(wt[:, ring, i, f:l], wt[:, ring, i, f:l], ACT.Exp,
                                             bias=low[:, ring, i:i + 1], scale=-1.0,
                                             accum_out=total[:, c, i, j:j + 1])
                    if half:
                        ins.then_inc(s_exp, 1)

                def hi_of_weights(b, k, fresh):
                    m = heads * b + k
                    if not fresh:
                        wait(act, s_pv, m - 1)
                    for h in range(2):
                        wait(act, s_t, 2 * m + h + 1)
                        act.activation(pt[:, k % 2, 0, h], ps[:, bank_t[h], :], ACT.Copy).then_inc(s_phi, 1)

                def inverse_out(u, fresh):
                    wait(act, s_invt, u + 1)
                    if not fresh:
                        wait(act, s_alo, u)
                    act.activation(inv_t[:], ps[:, bank_m, :], ACT.Copy).then_inc(s_invs, 1)

                def hi_of_output(u, c, fresh):
                    wait(act, s_a, u + 1)
                    if not fresh:
                        wait(act, s_proj, u - c)
                    act.activation(a_hi[:, c], inv_t[:], ACT.Copy).then_inc(s_ahi, 1)

                hi_of_q(0, 0)
                hi_of_k(0, 0)
                hi_of_values(0, 0)
                exponentials(0, 0, 0)
                exponentials(0, 0, 1)
                exponentials(0, 1, 0)

                def batch(b, first):
                    for n in range(heads):
                        hi_of_weights(b, n, first and n < 2)
                        exponentials(b, n + 1, 1)
                        if n % HC == 0 and not (first and n == 0):
                            inverse_out(2 * b + n // HC - 1, first and n == HC)
                        if n % HC == 1 and not (first and n == 1):
                            hi_of_output(2 * b + n // HC - 1, (n // HC - 1) % DC, first)
                        if n % HC == HC - 5:
                            hi_of_k(b, n + 5)
                        if n % HC == HC - 4:
                            hi_of_q(b, n + 4)
                        if first and n == 2:
                            wait(act, s_in, 32)
                            act.activation(wo_hi[:], wo_raw, ACT.Copy).then_inc(s_wohi, 1)
                        exponentials(b, n + 2, 0)
                        if n % HC == HC - 1:
                            hi_of_values(b, n + 1)

                each_batch(act, batch)
                inverse_out(2 * B - 1, False)
                hi_of_output(2 * B - 1, DC - 1, False)

            @block.tensor
            def _(pe):
                start(pe, by["pe"])

                def scores(b, k, fresh=False):
                    m, c, ring = heads * b + k, k // HC % DC, k % 2
                    wait(pe, s_qm, m + 1)
                    if not fresh:
                        wait(pe, s_low, 2 * m - 2)
                    if k % HC == 0:
                        wait(pe, s_klo, 2 * b + k // HC + 1)
                    for i in range(TB):
                        f, l, key = window(i)
                        for p, (a, kk) in enumerate(((0, 0), (0, 1), (1, 0))):
                            ins = pe.matmul(ps[:, bank_s[ring][i // 2], W * (i % 2) + f:W * (i % 2) + l],
                                            q_m[:, ring, a, i * P:(i + 1) * P],
                                            k_s[:, c, kk, key:key + l - f], start=(p == 0), stop=(p == 2))
                    ins.then_inc(s_s, 1)

                def transposes(b, k, fresh):
                    m, ring = heads * b + k, k % 2
                    wait(pe, s_exp, m + 1)
                    for i in range(TB):
                        if i % 2 == 0 and not fresh:
                            wait(pe, s_plo, 2 * m + i // 2 - 1)
                        for h in range(2):
                            at = (2 * i + h) % TB
                            ins = pe.transpose(ps[:, bank_t[i // 2], at * P:(at + 1) * P],
                                               wt[:, ring, i, h * P:(h + 1) * P], g.ident[:])
                        if i % 2:
                            ins.then_inc(s_t, 1)

                def weighted_values(b, k):
                    m, j, ring = heads * b + k, k % HC, k % 2
                    wait(pe, s_vm, m + 1)
                    wait(pe, s_plo, 2 * m + 2)
                    if j == 0:
                        wait(pe, s_a, 2 * b + k // HC)
                    hi = pt[:, ring, 0].rearrange("p h n -> p (h n)")
                    lo = pt[:, ring, 1].rearrange("p h n -> p (h n)")
                    for t in range(VT):
                        a, z = max(0, (2 * t - 1) * P), min(2 * N, (2 * t + 1) * P)
                        o = max(0, (t - 1) * P)
                        for p, (vv, w) in enumerate(((0, hi), (0, lo), (1, hi))):
                            ins = pe.matmul(ps[:, bank_o, o:o + z - a], v_m[:, ring, vv, t, :], w[:, a:z],
                                            start=(j == 0 and t == 0 and p == 0),
                                            stop=(j == HC - 1 and t == VT - 1 and p == 2),
                                            skip_group_check=True)
                    ins.then_inc(s_pv, 1)

                def transpose_inverse(u):
                    wait(pe, s_inv, u + 1)
                    for i in range(TB):
                        ins = pe.transpose(ps[:, bank_m, i * P:(i + 1) * P],
                                           inv[:, i].rearrange("p h d -> p (h d)"), g.ident[:])
                    ins.then_inc(s_invt, 1)

                def project(b, h, bank=bank_m):
                    wait(pe, s_wolo, 1)
                    wait(pe, s_alo, 2 * b + 2)
                    if bank == bank_m:
                        wait(pe, s_done, 2 * b + h)
                    for t in range(2):
                        k = 0
                        tok = (2 * h + t) * P
                        for c in range(DC):
                            for a, w in ((a_hi, wo_hi), (a_lo, wo_hi), (a_hi, wo_lo)):
                                ins = pe.matmul(ps[:, bank, t * D:(t + 1) * D], a[:, c, tok:tok + P],
                                                w[:, c, :], start=(k == 0), stop=(k == 5))
                                k += 1
                    ins.then_inc(s_proj, 1)

                scores(0, 0, True)
                scores(0, 1, True)
                wait(pe, s_const, 6)

                def batch(b, first):
                    for n in range(heads):
                        after_first = not (first and n == 0)
                        transposes(b, n, not after_first)
                        if n % HC == 0 and after_first:
                            transpose_inverse(2 * b + n // HC - 1)
                        scores(b, n + 2)
                        if after_first:
                            weighted_values(b, n - 1)
                        if n in (2, 4) and not first:
                            project(b - 1, (n - 2) // 2)

                each_batch(pe, batch)
                transpose_inverse(2 * B - 1)
                weighted_values(B - 1, heads - 1)
                project(B - 1, 0)
                project(B - 1, 1, bank_t[0])


def experts(nc, g):
    with ExitStack() as ctx:
        def sb(name, shape, dt=F32):
            return ctx.enter_context(nc.sbuf_tensor(name, shape, dt))

        by = {"sp": [], "pool": [], "v": [], "act": [], "pe": []}

        def sem(name, engine):
            by[engine].append(ctx.enter_context(nc.semaphore(name)))
            return by[engine][-1]

        def dma_sem(name):
            return ctx.enter_context(nc.semaphore(name))

        ps = ctx.enter_context(nc.psum_tensor("ps_experts", [P, 8, 512], F32))
        w1_hi = sb("w1_hi", [P, DC, F], F32R)
        w1_lo = sb("w1_lo", [P, DC, F], F32R)
        w2_hi = sb("w2_hi", [P, FC, D], F32R)
        w2_lo = sb("w2_lo", [P, FC, D], F32R)
        b1 = sb("b1_s", [P, E * FC])
        b2 = sb("b2_s", [P, E, D])
        index = sb("index", [P, RING, 2], U32)
        target = sb("target", [P, 2], U32)
        xg = sb("xg", [P, RING, 2, D])
        xt_hi = sb("xgt_hi", [P, DC, ROWS], F32R)
        xt_lo = sb("xgt_lo", [P, DC, ROWS], F32R)
        hid = sb("hid", [P, 2, 2, ROWS])
        h_hi = sb("h_hi", [P, FC, ROWS], F32R)
        h_lo = sb("h_lo", [P, FC, ROWS], F32R)
        gated_b2 = sb("gated_b2", [P, 2, D])
        y = sb("y", [P, 2, D])

        s_b1 = sem("s_b1", "sp")
        s_b2 = sem("s_b2", "sp")
        s_last = sem("s_last", "sp")
        s_landed = sem("s_landed", "sp")
        s_idx = sem("s_idx", "pool")
        s_g = [dma_sem("s_g0"), dma_sem("s_g1")]
        s_tr = sem("s_tr4", "pe")
        s_xhi = sem("s_xhi", "act")
        s_xlo = sem("s_xlo", "v")
        s_w1hi = sem("s_w1hi", "act")
        s_w1lo = sem("s_w1lo", "v")
        s_w2hi = sem("s_w2hi", "act")
        s_w2lo = sem("s_w2lo", "v")
        s_l1 = sem("s_l1", "pe")
        s_hid = sem("s_hid", "act")
        s_hhi = sem("s_hhi", "v")
        s_h = sem("s_h", "v")
        s_l2 = sem("s_l2", "pe")
        s_y = sem("s_y", "v")
        s_target = sem("s_target", "pool")
        s_gated = sem("s_gated", "act")
        s_sum = [dma_sem("s_sum0"), dma_sem("s_sum1")]
        s_summed = sem("s_summed", "pool")

        bank_h, bank_t, bank_y = (0, 1, 2, 3), 4, (5, 6)
        FG, MG = F // 2, FC // 2
        out_tokens = g.out.rearrange("b n d -> (b n) d")

        def expert_of(eng, s):
            return eng.value_load(g.step_expert[0:1, ds(s, 1)], min_val=0, max_val=E - 1)

        with nc.Block() as block:
            @block.sync
            def _(sp):
                start(sp, by["sp"])
                sp.dma_start(b1[:], g.b1_cols).then_inc(s_b1, 16)
                wait(sp, s_tr, 1)
                sp.dma_start(b2[:], g.b2.partition_broadcast(P)).then_inc(s_b2, 16)
                wait(sp, s_b2, 16)
                wait(sp, s_tr, 4)
                sp.dma_start(g.w1_of(E - 1), g.w1[E - 1].rearrange("(c p) f -> p c f", p=P)).then_inc(s_last, 16)
                wait(sp, s_tr, 6)
                sp.dma_start(g.w2_of(E - 1), g.w2[E - 1].rearrange("(m p) d -> p m d", p=P)).then_inc(s_last, 16)
                wait(sp, s_last, 32)
                sp.sem_inc(s_landed, 2)

            @block.gpsimd
            def _(pool):
                start(pool, by["pool"])

                def gather(s, row_step, ring):
                    pool.tensor_copy(index[:, ring], g.rows[:, ds(2 * row_step, 2), 0].bitcast(U32)).then_inc(s_idx, 1)
                    wait_first(pool, s_idx, s + 1, g.tick)
                    for h in range(2):
                        pool.indirect_dma_start(
                            xg[:, ring, h], None, g.xn_dram,
                            bass.IndirectOffsetOnAxis(ap=index[:, ring, h:h + 1], axis=0)
                            ).then_inc(s_g[h], 16)

                gather(0, 0, 0)
                for h in range(2):
                    pool.wait_ge(s_g[h], 16)
                gather(1, 1, 1)
                with pool.Fori(0, STEPS // RING) as trip:
                    for turn in range(RING):
                        s = RING * trip + turn
                        for h in range(2):
                            pool.wait_ge(s_g[h], 16 * s + 32)
                            pool.sem_inc(g.tick, 1)
                        wait_first(pool, s_tr, s, g.tick)
                        gather(s + 2, (s + 2) % STEPS, (turn + 2) % RING)
                        pool.tensor_copy(target[:], g.rows[:, ds(2 * s, 2), 0].bitcast(U32)).then_inc(s_target, 1)
                        wait_first(pool, s_target, s + 1, g.tick)
                        wait_first(pool, s_y, s + 1, g.tick)
                        for h in range(2):
                            pool.indirect_dma_start(
                                out_tokens, bass.IndirectOffsetOnAxis(ap=target[:, h:h + 1], axis=0),
                                y[:, h], None, compute_op=ALU.add).then_inc(s_sum[h], 16)
                        for h in range(2):
                            pool.wait_ge(s_sum[h], 16 * s + 16)
                            pool.sem_inc(s_summed if h else g.tick, 1)
                for h in range(2):
                    pool.wait_ge(s_g[h], 16 * (STEPS + 2))

            @block.vector
            def _(v):
                start(v, by["v"])

                def lo_of_w1(s, e, n):
                    wait(v, s_w1hi, 2 * s + n + 1)
                    cols = slice(n * FG, (n + 1) * FG)
                    v.tensor_tensor(w1_lo[:, :, cols], g.w1_of(e)[:, :, cols], w1_hi[:, :, cols].bitcast(F32),
                                    ALU.subtract).then_inc(s_w1lo, 1)

                def lo_of_w2(s, e, n):
                    wait(v, s_w2hi, 2 * s + n + 1)
                    m = slice(n * MG, (n + 1) * MG)
                    v.tensor_tensor(w2_lo[:, m], g.w2_of(e)[:, m], w2_hi[:, m].bitcast(F32),
                                    ALU.subtract).then_inc(s_w2lo, 1)

                def lo_of_rows(s):
                    wait(v, s_xhi, s + 1)
                    v.tensor_tensor(xt_lo[:].rearrange("p c n -> p (c n)"), ps[:, bank_t, :],
                                    xt_hi[:].rearrange("p c n -> p (c n)").bitcast(F32),
                                    ALU.subtract).then_inc(s_xlo, 1)

                def hidden(s, n):
                    wait(v, s_hid, 4 * s + n + 1)
                    v.tensor_copy(h_hi[:, 2 * n:2 * n + 2], hid[:, n % 2]).then_inc(s_hhi, 1)
                    wait(v, s_hhi, 4 * s + n + 1)
                    v.tensor_tensor(h_lo[:, 2 * n:2 * n + 2], hid[:, n % 2],
                                    h_hi[:, 2 * n:2 * n + 2].bitcast(F32), ALU.subtract).then_inc(s_h, 1)

                first = expert_of(v, 0)
                lo_of_w1(0, first, 0)
                lo_of_rows(0)
                lo_of_w1(0, first, 1)
                lo_of_w2(0, first, 0)
                with v.Fori(0, STEPS // RING) as trip:
                    for turn in range(RING):
                        s = RING * trip + turn
                        e, e_next = expert_of(v, s), expert_of(v, (s + 1) % STEPS)
                        hidden(s, 0)
                        hidden(s, 1)
                        lo_of_w2(s, e, 1)
                        hidden(s, 2)
                        hidden(s, 3)
                        wait_first(v, s_landed, (s + 1) // (T // ROWS), g.tick)
                        lo_of_w1(s + 1, e_next, 0)
                        lo_of_rows(s + 1)
                        lo_of_w1(s + 1, e_next, 1)
                        lo_of_w2(s + 1, e_next, 0)
                        wait(v, s_l2, 2 * s + 2)
                        wait(v, s_gated, s + 1)
                        wait_first(v, s_summed, s, g.tick)
                        for h in range(2):
                            ins = v.scalar_tensor_tensor(
                                out=y[:, h], in0=ps[:, bank_y[h], 0:D], scalar=g.rows[:, ds(2 * s + h, 1), 1],
                                in1=gated_b2[:, h], op0=ALU.mult, op1=ALU.add)
                        ins.then_inc(s_y, 1)

            @block.scalar
            def _(act):
                start(act, by["act"])

                def hi_of_w1(e, n):
                    cols = slice(n * FG, (n + 1) * FG)
                    act.activation(w1_hi[:, :, cols], g.w1_of(e)[:, :, cols], ACT.Copy).then_inc(s_w1hi, 1)

                def hi_of_w2(e, n):
                    m = slice(n * MG, (n + 1) * MG)
                    act.activation(w2_hi[:, m], g.w2_of(e)[:, m], ACT.Copy).then_inc(s_w2hi, 1)

                def hi_of_rows(s):
                    wait_first(act, s_tr, s + 1, g.tick)
                    act.activation(xt_hi[:].rearrange("p c n -> p (c n)"), ps[:, bank_t, :], ACT.Copy
                                   ).then_inc(s_xhi, 1)

                def hidden(s, e, n):
                    wait_first(act, s_l1, 4 * s + n + 1, g.tick)
                    wait_first(act, s_h, 4 * s + n - 1 if n > 1 else 4 * s, g.tick)
                    for j in range(2):
                        ins = act.activation(hid[:, n % 2, j], ps[:, bank_h[n], j * ROWS:(j + 1) * ROWS],
                                             ACT.Relu, bias=b1[:, ds(e * FC + 2 * n + j, 1)])
                    ins.then_inc(s_hid, 1)

                def gated_bias(s, e):
                    wait(act, s_b2, 16)
                    wait_first(act, s_y, s, g.tick)
                    for h in range(2):
                        ins = act.activation(gated_b2[:, h], b2[:, ds(e, 1), :], ACT.Copy,
                                             scale=g.rows[:, ds(2 * s + h, 1), 1])
                    ins.then_inc(s_gated, 1)

                first = expert_of(act, 0)
                hi_of_w1(first, 0)
                hi_of_rows(0)
                hi_of_w1(first, 1)
                hi_of_w2(first, 0)
                wait(act, s_b1, 16)
                with act.Fori(0, STEPS // RING) as trip:
                    for turn in range(RING):
                        s = RING * trip + turn
                        e, e_next = expert_of(act, s), expert_of(act, (s + 1) % STEPS)
                        hidden(s, e, 0)
                        hi_of_w2(e, 1)
                        hidden(s, e, 1)
                        hidden(s, e, 2)
                        hidden(s, e, 3)
                        wait_first(act, s_landed, (s + 1) // (T // ROWS), g.tick)
                        hi_of_w1(e_next, 0)
                        hi_of_rows(s + 1)
                        hi_of_w1(e_next, 1)
                        gated_bias(s, e)
                        wait_first(act, s_l2, 2 * s + 1, g.tick)
                        hi_of_w2(e_next, 0)

            @block.tensor
            def _(pe):
                start(pe, by["pe"])

                def transpose_rows(s, ring):
                    for h in range(2):
                        pe.wait_ge(s_g[h], 16 * s + 16)
                    wait(pe, s_xlo, s)
                    for c in range(DC):
                        for h in range(2):
                            ins = pe.transpose(ps[:, bank_t, (c * 2 + h) * P:(c * 2 + h + 1) * P],
                                               xg[:, ring, h, c * P:(c + 1) * P], g.ident[:])
                    ins.then_inc(s_tr, 1)

                transpose_rows(0, 0)
                with pe.Fori(0, STEPS // RING) as trip:
                    for turn in range(RING):
                        s = RING * trip + turn
                        wait(pe, s_xlo, s + 1)
                        wait(pe, s_hid, 4 * s)
                        for m in range(FC):
                            if m % MG == 0:
                                wait(pe, s_w1lo, 2 * s + m // MG + 1)
                            k = 0
                            for c in range(DC):
                                for w, xx in ((w1_hi, xt_hi), (w1_hi, xt_lo), (w1_lo, xt_hi)):
                                    ins = pe.matmul(ps[:, bank_h[m // 2], m % 2 * ROWS:(m % 2 + 1) * ROWS],
                                                    w[:, c, m * P:(m + 1) * P], xx[:, c, :],
                                                    start=(k == 0), stop=(k == 5))
                                    k += 1
                            if m % 2:
                                ins.then_inc(s_l1, 1)
                        wait(pe, s_y, s)
                        transpose_rows(s + 1, (turn + 1) % RING)
                        for m in range(FC):
                            if m % MG == 0:
                                wait(pe, s_w2lo, 2 * s + m // MG + 1)
                            if m % 2 == 0:
                                wait(pe, s_h, 4 * s + m // 2 + 1)
                            for h in range(2):
                                for k, (a, w) in enumerate(((h_hi, w2_hi), (h_lo, w2_hi), (h_hi, w2_lo))):
                                    ins = pe.matmul(ps[:, bank_y[h], 0:D], a[:, m, h * P:(h + 1) * P], w[:, m, :],
                                                    start=(m == 0 and k == 0), stop=(m == FC - 1 and k == 2))
                            if m % MG == MG - 1:
                                ins.then_inc(s_l2, 1)


def build(nc, g):
    with ExitStack() as ctx:
        def sb(name, shape, dt=F32):
            return ctx.enter_context(nc.sbuf_tensor(name, shape, dt))

        g.xn_dram = nc.dram_tensor("xn_rows", (T, D), F32).ap()
        g.table_dram = nc.dram_tensor("table", (SLOTS, 2), F32).ap()
        per_expert = DC * F + FC * D
        per_batch = 2 * DC * N + VT * D
        g.pool = sb("weights_qkv", [P, E * per_expert])
        qkv_at = E * per_expert - B * per_batch
        g.ident = sb("ident", [P, P])
        g.entry = sb("entry", [P, NT, E, 2])
        g.entry_at = sb("entry_at", [P, NT, E], U32)
        g.logits = g.entry_at[:].bitcast(F32)
        g.rows = sb("rows", [P, HT, 2])
        g.step_expert = sb("step_expert", [P, STEPS], I32)

        per_chunk = per_batch // DC

        def q_of(b, c):
            return g.pool[:, ds(b * per_batch + qkv_at + c * per_chunk, N)]

        def k_of(b, c):
            return g.pool[:, ds(b * per_batch + qkv_at + c * per_chunk + N, N)]

        def v_chunk(b, c):
            return g.pool[:, ds(b * per_batch + qkv_at + c * per_chunk + 2 * N, VT * P)].rearrange(
                "p (t d) -> p t d", d=P)

        def v_of(b, c, t, n):
            return g.pool[:, ds(b * per_batch + qkv_at + c * per_chunk + 2 * N + t * P, n * P)].rearrange(
                "p (t d) -> p t d", d=P)

        def w1_of(e):
            return g.pool[:, ds(e * per_expert, DC * F)].rearrange("p (c f) -> p c f", c=DC)

        def w2_of(e):
            return g.pool[:, ds(e * per_expert + DC * F, FC * D)].rearrange("p (m d) -> p m d", m=FC)

        g.q_of, g.k_of, g.v_of, g.v_chunk, g.w1_of, g.w2_of = q_of, k_of, v_of, v_chunk, w1_of, w2_of
        g.tick = ctx.enter_context(nc.semaphore("tick"))
        norm_project(nc, g)
        route(nc, g)
        attend(nc, g)
        experts(nc, g)


def lay_out(inputs):
    import numpy as np

    arrays = {name.split("_", 2)[2]: np.ascontiguousarray(a) for name, a in inputs.items()}
    arrays["bqk_cols"] = np.ascontiguousarray(arrays["bqkv"][:2 * D].reshape(2 * DC, P).T)
    arrays["b1_cols"] = np.ascontiguousarray(arrays["b1"].reshape(E * FC, P).T)
    return arrays


def kernel(**inputs):
    import concourse.bacc as bacc
    from concourse.bass_utils import run_bass_kernel_spmd

    nc = bacc.Bacc("TRN2", target_bir_lowering=False, num_devices=1)
    arrays = lay_out(inputs)
    g = Shared({
        name: nc.dram_tensor(f"in_{name}", a.shape, mybir.dt.from_np(a.dtype), kind="ExternalInput").ap()
        for name, a in arrays.items()})
    g.out = nc.dram_tensor("out", (B, N, D), F32, kind="ExternalOutput").ap()
    build(nc, g)
    run = run_bass_kernel_spmd(nc, [{f"in_{name}": a for name, a in arrays.items()}], core_ids=[0])
    return run.results[0]["out"]
```
